# Optimizing a Trainium2 kernel written in Bass

```python
import numpy as np
import jax
import jax.numpy as jnp

def _softmax(x, axis=-1):
    return jax.nn.softmax(x, axis=axis)

def _gelu(x):
    return jax.nn.gelu(x, approximate=True)

def _silu(x):
    return jax.nn.silu(x)

def _sigmoid(x):
    return jax.nn.sigmoid(x)

def _layernorm(x, axis=-1, eps=1e-05):
    m = jnp.mean(x, axis=axis, keepdims=True)
    v = jnp.var(x, axis=axis, keepdims=True)
    return (x - m) / jnp.sqrt(v + eps)

def _scatter_add(tgt, idx, src, axis=0):
    return tgt.at[idx].add(src)

def _segment_sum(src, seg, n):
    return jax.ops.segment_sum(src, seg, n)
kernel_name = 'mk_prb_d1_jaxref_r4_80b870'

def setup_inputs(seed: int=0):
    np.random.seed(seed)
    _w = jnp.asarray

    def _L0_attn_setup():
        import jax, jax.numpy as jnp
        import numpy as np
        HEADS = 32
        key = jax.random.key(seed)
        ks = jax.random.split(key, 5)
        H = 1024
        B, S = (2, 512)
        w_scale = 1.0 / np.sqrt(H)
        return {'x': jax.random.normal(ks[0], (B, S, H), dtype=jnp.float32), 'attn_qkvw': jax.random.normal(ks[1], (H, 3 * H), dtype=jnp.float32) * w_scale, 'attn_qkvb': jax.random.normal(ks[2], (3 * H,), dtype=jnp.float32) * 0.02, 'attn_ow': jax.random.normal(ks[3], (H, H), dtype=jnp.float32) * w_scale, 'attn_ob': jax.random.normal(ks[4], (H,), dtype=jnp.float32) * 0.02}
    _L0_attn_in = _L0_attn_setup()

    def _L0_ffn_setup():
        import jax, jax.numpy as jnp
        import numpy as np
        IN_F = 1024
        OUT_F = 1024
        RANK = 8
        NUM_EXPERTS = 64
        TOP_K = 16
        ROUTER_DIM = 16
        ALPHA = 32
        SCALING = ALPHA / TOP_K
        BOTTLENECK = NUM_EXPERTS * RANK
        key = jax.random.key(seed)
        ks = jax.random.split(key, 5)
        x = jax.random.normal(ks[0], (4, 1024, IN_F), dtype=jnp.float32)
        bound_a = float(np.sqrt(6.0 / IN_F))
        A_w = jax.random.uniform(ks[1], (BOTTLENECK, IN_F), jnp.float32, -bound_a, bound_a)
        B_w = jax.random.normal(ks[2], (OUT_F, BOTTLENECK), dtype=jnp.float32) * 0.02
        Wq_w = jax.random.normal(ks[3], (ROUTER_DIM, IN_F), dtype=jnp.float32) * 0.02
        keys = jax.random.normal(ks[4], (NUM_EXPERTS, ROUTER_DIM), dtype=jnp.float32) * 0.01
        return {'x': x, 'A_w': A_w, 'B_w': B_w, 'Wq_w': Wq_w, 'keys': keys}
    _L0_ffn_in = _L0_ffn_setup()
    _d = {'L0_attn_x': _L0_attn_in['x'], 'L0_attn_attn_qkvw': _L0_attn_in['attn_qkvw'], 'L0_attn_attn_qkvb': _L0_attn_in['attn_qkvb'], 'L0_attn_attn_ow': _L0_attn_in['attn_ow'], 'L0_attn_attn_ob': _L0_attn_in['attn_ob'], 'L0_ffn_A_w': _L0_ffn_in['A_w'], 'L0_ffn_B_w': _L0_ffn_in['B_w'], 'L0_ffn_Wq_w': _L0_ffn_in['Wq_w'], 'L0_ffn_keys': _L0_ffn_in['keys']}
    _x0 = _d['L0_attn_x']
    _d['L0_attn_x'] = jax.random.normal(jax.random.fold_in(jax.random.key(seed), 1), (1, 2048, 1024), dtype=_x0.dtype)
    del _x0
    return _d

def reference(L0_attn_x, L0_attn_attn_qkvw, L0_attn_attn_qkvb, L0_attn_attn_ow, L0_attn_attn_ob, L0_ffn_A_w, L0_ffn_B_w, L0_ffn_Wq_w, L0_ffn_keys):

    def _L0_attn_ref(x, attn_qkvw, attn_qkvb, attn_ow, attn_ob):
        import jax, jax.numpy as jnp
        import numpy as np
        HEADS = 32
        B, S, H = x.shape
        hd = H // HEADS
        scale = 1.0 / np.sqrt(hd)
        qkv = x @ attn_qkvw + attn_qkvb
        qkv = qkv.reshape(B, S, 3, HEADS, hd)
        q = jnp.transpose(qkv[:, :, 0], (0, 2, 1, 3))
        k = jnp.transpose(qkv[:, :, 1], (0, 2, 1, 3))
        v = jnp.transpose(qkv[:, :, 2], (0, 2, 1, 3))
        scores = jnp.einsum('bhqd,bhkd->bhqk', q, k) * scale
        probs = jax.nn.softmax(scores, axis=-1)
        ctx = jnp.einsum('bhqk,bhkd->bhqd', probs, v)
        ctx = jnp.transpose(ctx, (0, 2, 1, 3)).reshape(B, S, H)
        return ctx @ attn_ow + attn_ob

    def _L0_ffn_ref(x, A_w, B_w, Wq_w, keys):
        import jax, jax.numpy as jnp
        import numpy as np
        IN_F = 1024
        OUT_F = 1024
        RANK = 8
        NUM_EXPERTS = 64
        TOP_K = 16
        ROUTER_DIM = 16
        ALPHA = 32
        SCALING = ALPHA / TOP_K
        BOTTLENECK = NUM_EXPERTS * RANK
        q = jnp.einsum('bsd,rd->bsr', x, Wq_w)
        scores = jnp.einsum('bsr,er->bse', q, keys)
        top_vals, top_idx = jax.lax.top_k(scores, TOP_K)
        top_w = jax.nn.softmax(top_vals, axis=-1)
        gate = jnp.sum(jax.nn.one_hot(top_idx, NUM_EXPERTS, dtype=top_w.dtype) * top_w[..., None], axis=-2)
        z = jnp.einsum('bsd,nd->bsn', x, A_w)
        z = z.reshape(*z.shape[:-1], NUM_EXPERTS, RANK)
        z_gated = (z * gate[..., None]).reshape(*z.shape[:-2], BOTTLENECK)
        out = jnp.einsum('bsn,on->bso', z_gated, B_w) * SCALING
        return out
    x = L0_attn_x
    xn = _layernorm(x, axis=-1)
    x = x + _L0_attn_ref(xn, L0_attn_attn_qkvw, L0_attn_attn_qkvb, L0_attn_attn_ow, L0_attn_attn_ob) + _L0_ffn_ref(xn, L0_ffn_A_w, L0_ffn_B_w, L0_ffn_Wq_w, L0_ffn_keys)
    return x

_drawn_inputs = setup_inputs


def setup_inputs(seed=0):
    import zlib

    import numpy as np

    out = dict(_drawn_inputs(seed))
    spreads = {}
    factors = {'L0_attn_attn_qkvb': 2.833, 'L0_attn_attn_ob': 2.885}
    for name, (base, spread) in spreads.items():
        noise = np.random.default_rng([zlib.crc32(name.encode()), seed]).standard_normal(out[name].shape)
        drawn = base * np.exp(spread * noise) if base else spread * noise
        out[name] = jnp.asarray(drawn.astype(out[name].dtype))
    for name, factor in factors.items():
        out[name] = (out[name] * factor).astype(out[name].dtype)
    return out
```

```python
from contextlib import ExitStack

import concourse.bass as bass
from concourse import mybir

F32 = mybir.dt.float32
F32R = mybir.dt.float32r
ALU = mybir.AluOpType
ACT = mybir.ActivationFunctionType
AX_X = mybir.AxisListType.X

P = 128
T = 2048
D = 1024
HEADS = 32
HD = D // HEADS
SCALE = HD ** -0.5
EPS = 1e-5
KT = D // P
TT = T // P
NQ = 512
QB = T // NQ
EXPERTS = 64
RANK = 8
BOTTLENECK = EXPERTS * RANK
ROUTER = 16
SCALING = 2.0
LOWEST = -3.0e38

ROUTER_BLOCK = 0
QK_BLOCKS = 2 * D // P
V_BLOCKS = D // P
Z_BLOCKS = BOTTLENECK // P
V0 = 1 + QK_BLOCKS
Z0 = V0 + V_BLOCKS
BLOCKS = Z0 + Z_BLOCKS
WROW = KT * P + 1

PACK = 3 * HD

POOL_TILES = [0, 1, 2, 4, 6, 7, 8, 10, 11, 12]
DVE_TILES = [3, 5, 9]
PE_TILES = [t for t in range(TT) if t not in POOL_TILES + DVE_TILES]
POOL_OPS = len(POOL_TILES)
DVE_OPS = 2 * (len(DVE_TILES) - 1)
RECIPROCAL_AT, NORMALISE_AT = 7, 10
ADD_AT = [6, 8, 11, 13]
RING = 8
SLOTS = 4

OUT_KT = KT + Z_BLOCKS


def wait(eng, sem, value):
    if isinstance(value, int) and value <= 0:
        return
    eng.wait_ge(sem, value)


def project_inputs(nc, x, wcat, keys_t, qk_scr, v_scr, gate_scr, cz_scr):
    with ExitStack() as ctx:
        def sb(name, shape, dt=F32):
            return ctx.enter_context(nc.sbuf_tensor(name, shape, dt))

        def sem(name):
            return ctx.enter_context(nc.semaphore(name))

        xhi = sb("xhi", [P, KT, T], F32R)
        xlo = sb("xlo", [P, KT, T], F32R)
        wraw = sb("wraw", [P, 2, WROW])
        whi = sb("whi", [P, 2, KT * P], F32R)
        wlo = sb("wlo", [P, 2, KT * P], F32R)
        ehi = sb("ehi", [P, 2, T])
        elo = sb("elo", [P, 2, T])
        stage = sb("stage", [P, 2 * T])
        ident = sb("ident", [P, P])
        keys = sb("keys", [ROUTER, EXPERTS])
        stats = sb("stats", [P, 2, 2, 6])
        mv = sb("mv", [P, 2, 2])
        std = sb("std", [P, 2, 2])
        top = sb("top", [P, TT, 16])
        gsum = sb("gsum", [P, TT, 2])
        ps = ctx.enter_context(nc.psum_tensor("ps_a", [P, 8, NQ], F32))

        x_in = stage[:, 0:2 * D].rearrange("p (u d) -> p u d", u=2)
        xn = stage[:, 2 * D:4 * D].rearrange("p (u d) -> p u d", u=2)
        qr_t = stage[0:ROUTER, 0:T]
        sc_flat = stage[:, T:T + TT * EXPERTS]
        sc = sc_flat.rearrange("p (t e) -> p t e", e=EXPERTS)
        left_flat = stage[:, T + TT * EXPERTS:T + 2 * TT * EXPERTS]
        left = left_flat.rearrange("p (t e) -> p t e", e=EXPERTS)
        gate_t = stage[0:EXPERTS, 0:T]
        gates = stage[:, :].rearrange("p (u t) -> p u t", u=2)

        x_loaded = [sem("x_loaded0"), sem("x_loaded1")]
        ident_done = sem("ident_done")
        keys_loaded = sem("keys_loaded")
        stats_done = sem("stats_done")
        stats_seen = sem("stats_seen")
        mean_done = sem("mean_done")
        var_ready = sem("var_ready")
        std_ready = sem("std_ready")
        rstd_done = sem("rstd_done")
        xn_ready = sem("xn_ready")
        xt_ready = sem("xt_ready")
        xhi_done = sem("xhi_done")
        xlo_done = sem("xlo_done")
        w_loaded = [sem("w_loaded0"), sem("w_loaded1")]
        whi_done = sem("whi_done")
        wlo_done = sem("wlo_done")
        mm_ready = sem("mm_ready")
        hi_done = sem("hi_done")
        lo_done = sem("lo_done")
        stored = [sem("stored0"), sem("stored1")]
        score_ready = sem("score_ready")
        top_step = sem("top_step")
        shifted_ready = sem("shifted_ready")
        gexp_ready = sem("gexp_ready")
        gate_ready = sem("gate_ready")
        gtr_ready = sem("gtr_ready")
        gate_t_ready = sem("gate_t_ready")
        gate_stored = sem("gate_stored")
        gates_loaded = [sem("gates_loaded0"), sem("gates_loaded1")]
        vtr_ready = sem("vtr_ready")

        def quarter(blk, nb):
            return 4 * blk + nb + 1

        def hi_count(blk, nb):
            return 4 * blk + nb - 3

        def pair(i):
            return [(u, 2 * i + u + 1) for u in range(2)]

        block = ctx.enter_context(nc.Block())

        @block.sync
        def _(sp):
            def load_w(blk, slot):
                sp.dma_start(wraw[:, slot, :], wcat[bass.ds(blk, 1), :, :].rearrange("a p n -> (a p) n")) \
                    .then_inc(w_loaded[slot], 16)

            def load_gates(b, u):
                for r in range(RANK):
                    sp.dma_start(gates[r::RANK, u, :], gate_scr[16 * b:16 * b + 16, :]) \
                        .then_inc(gates_loaded[u], 16)

            def store_qk(blk, u):
                row = (blk - 1) * P
                for part, ev in ((0, ehi), (1, elo)):
                    sp.dma_start(qk_scr[part, bass.ds(row, P), :], ev[:, u, :]).then_inc(stored[u], 16)

            sp.dma_start(keys[:, :], keys_t).then_inc(keys_loaded, 16)
            load_w(0, 0)
            load_w(1, 1)
            for u in range(2):
                sp.dma_start(x_in[:, u, :], x[u * P:(u + 1) * P, :]).then_inc(x_loaded[u], 16)
            with sp.Fori(1, TT // 2) as i:
                for u in range(2):
                    sp.wait_ge(xn_ready, 2 * i + u - 1)
                    sp.dma_start(x_in[:, u, :], x[bass.ds((2 * i + u) * P, P), :]).then_inc(x_loaded[u], 16)
            sp.wait_ge(lo_done, quarter(0, 3))
            load_w(2, 0)

            def after_qk(i):
                for u, blk in pair(i):
                    sp.wait_ge(lo_done, quarter(blk, 3))
                    store_qk(blk, u)
                    load_w(blk + 2, (u + 1) % 2)

            after_qk(0)
            sp.wait_ge(gate_t_ready, 1)
            sp.dma_start(gate_scr, gate_t).then_inc(gate_stored, 16)
            with sp.Fori(1, QK_BLOCKS // 2) as i:
                after_qk(i)
            sp.wait_ge(gate_stored, 16)
            for u in range(2):
                load_gates(u, u)
            with sp.Fori(QK_BLOCKS // 2, (QK_BLOCKS + V_BLOCKS) // 2) as i:
                for u, blk in pair(i):
                    sp.wait_ge(lo_done, quarter(blk, 3))
                    vb = blk - V0
                    for half in range(2):
                        c = slice(half * T // 2, (half + 1) * T // 2)
                        sp.dma_start(v_scr[bass.ds(vb, 1), :, c].rearrange("a p n -> (a p) n"), elo[:, u, c]) \
                            .then_inc(stored[u], 16)
                    load_w(blk + 2, (u + 1) % 2)
            for b in range(Z_BLOCKS):
                blk, u = Z0 + b, b % 2
                sp.wait_ge(lo_done, quarter(blk, 3))
                for half in range(2):
                    c = slice(half * T // 2, (half + 1) * T // 2)
                    sp.dma_start(cz_scr[D + b * P:D + (b + 1) * P, c], elo[:, u, c]).then_inc(stored[u], 16)
                if blk + 2 < BLOCKS:
                    load_w(blk + 2, (u + 1) % 2)
                    load_gates(b + 2, u)
            for u in range(2):
                sp.wait_ge(stored[u], 32 * (BLOCKS - 1) // 2)

        @block.gpsimd
        def _(pool):
            pool.memset(ident[:, :], 0.0).then_inc(ident_done, 1)
            pool.wait_ge(ident_done, 1)
            pool.affine_select(out=ident[:, :], in_=ident[:, :], compare_op=ALU.not_equal, fill=1.0,
                               base=0, pattern=[[-1, P]], channel_multiplier=1).then_inc(ident_done, 1)

            def split(blk, slot):
                pool.wait_ge(whi_done, blk + 1)
                pool.tensor_tensor(wlo[:, slot, :], wraw[:, slot, 0:KT * P], whi[:, slot, :].bitcast(F32),
                                   ALU.subtract).then_inc(wlo_done, 1)

            split(0, 0)
            with pool.Fori(0, (BLOCKS - 1) // 2) as i:
                for u, blk in pair(i):
                    split(blk, (u + 1) % 2)

        @block.tensor
        def _(pe):
            pe.wait_ge(ident_done, 2)

            def transpose_x(i):
                for u in range(2):
                    pe.wait_ge(xn_ready, 2 * i + u + 1)
                    wait(pe, xlo_done, 2 * i + u - 1)
                    for k in range(KT):
                        last = pe.transpose(ps[:, 4 + 2 * u + k // 4, (k % 4) * P:(k % 4 + 1) * P],
                                            xn[:, u, k * P:(k + 1) * P], ident[:, :])
                    last.then_inc(xt_ready, 1)

            transpose_x(0)
            with pe.Fori(1, TT // 2) as i:
                transpose_x(i)
            pe.wait_ge(xhi_done, TT)
            pe.wait_ge(xlo_done, TT)

            def project(slot, nb):
                n = 0
                for k in range(KT):
                    wk = slice(k * P, (k + 1) * P)
                    tk = slice(nb * NQ, (nb + 1) * NQ)
                    for w, xx in ((whi, xhi), (whi, xlo), (wlo, xhi)):
                        last = pe.matmul(ps[:, nb, :], w[:, slot, wk], xx[:, k, tk],
                                         start=(n == 0), stop=(n == 3 * KT - 1))
                        n += 1
                last.then_inc(mm_ready, 1)

            def qk_block(u, blk):
                pe.wait_ge(wlo_done, blk + 1)
                for nb in range(QB):
                    wait(pe, lo_done, quarter(blk - 1, nb))
                    project((u + 1) % 2, nb)

            qk_block(1, 0)
            pe.wait_ge(lo_done, quarter(0, 3))
            pe.wait_ge(keys_loaded, 16)
            for t in range(TT):
                last = pe.matmul(ps[:, 6 + t // 8, (t % 8) * EXPERTS:(t % 8 + 1) * EXPERTS],
                                 qr_t[:, t * P:(t + 1) * P], keys[:, :], start=True, stop=True)
            last.then_inc(score_ready, 1)
            for u, blk in pair(0):
                qk_block(u, blk)
            pe.wait_ge(gate_ready, 1)
            for t in range(TT):
                last = pe.transpose(ps[0:EXPERTS, 4 + t // 4, (t % 4) * P:(t % 4 + 1) * P], sc[:, t, :], ident[:, :])
            last.then_inc(gtr_ready, 1)
            with pe.Fori(1, QK_BLOCKS // 2) as i:
                for u, blk in pair(i):
                    qk_block(u, blk)
            pe.wait_ge(gate_t_ready, 1)

            def transpose_v(u, blk, nb):
                pe.wait_ge(hi_done, hi_count(blk, nb))
                pe.wait_ge(lo_done, quarter(blk, nb) - 2)
                for t in range(4):
                    c = slice(nb * NQ + t * P, nb * NQ + (t + 1) * P)
                    last = pe.transpose(ps[:, 4 + nb % 2, t * P:(t + 1) * P], ehi[:, u, c], ident[:, :])
                last.then_inc(vtr_ready, 1)

            with pe.Fori(QK_BLOCKS // 2, (QK_BLOCKS + V_BLOCKS) // 2) as i:
                for u, blk in pair(i):
                    pe.wait_ge(wlo_done, blk + 1)
                    for nb in range(QB):
                        pe.wait_ge(lo_done, quarter(V0 - 1, nb))
                        pe.wait_ge(hi_done, hi_count(blk - 1, nb))
                        project((u + 1) % 2, nb)
                        if nb >= 1:
                            transpose_v(u, blk, nb - 1)
                    transpose_v(u, blk, QB - 1)
            for b in range(Z_BLOCKS):
                qk_block(b % 2, Z0 + b)

        @block.scalar
        def _(act):
            def round_w(blk, slot, loads):
                act.wait_ge(w_loaded[slot], 16 * loads)
                wait(act, mm_ready, quarter(blk - 2, 3))
                act.activation(whi[:, slot, :], wraw[:, slot, 0:KT * P], ACT.Copy).then_inc(whi_done, 1)

            round_w(0, 0, 1)
            round_w(1, 1, 1)

            def normalise(i):
                for u in range(2):
                    act.wait_ge(var_ready, 2 * i + u + 1)
                    act.activation(std[:, u, 0:1], mv[:, u, 1:2], ACT.Sqrt).then_inc(std_ready, 1)
                for u in range(2):
                    act.wait_ge(xt_ready, 2 * i + u + 1)
                    src = ps[:, 4 + 2 * u:6 + 2 * u, :].rearrange("p b (k n) -> p (b k) n", n=P)
                    act.activation(xhi[:, :, bass.ds((2 * i + u) * P, P)], src, ACT.Copy).then_inc(xhi_done, 1)

            with act.Fori(0, TT // 2) as i:
                normalise(i)
            act.wait_ge(shifted_ready, 1)
            act.activation(sc_flat, sc_flat, ACT.Exp).then_inc(gexp_ready, 1)

            def part(i, rounded):
                for u, blk in pair(i):
                    wait(act, stored[u], 32 * i)
                    for nb in range(QB):
                        if nb == 1:
                            round_w(blk + 1, u, i + 2)
                        c = slice(nb * NQ, (nb + 1) * NQ)
                        act.wait_ge(mm_ready, quarter(blk, nb))
                        dst = ehi[:, u, c].bitcast(F32R) if rounded else ehi[:, u, c]
                        act.activation(dst, ps[:, nb, :], ACT.Identity,
                                       bias=wraw[:, (u + 1) % 2, KT * P:WROW]).then_inc(hi_done, 1)

            part(0, True)
            with act.Fori(1, QK_BLOCKS // 2) as i:
                part(i, True)
            with act.Fori(QK_BLOCKS // 2, (QK_BLOCKS + V_BLOCKS) // 2) as i:
                part(i, False)
            for blk in range(Z0 + 1, BLOCKS):
                round_w(blk, blk % 2, blk // 2 + 1)

        @block.vector
        def _(dve):
            def normalise(i):
                for u in range(2):
                    dve.wait_ge(x_loaded[u], 16 * (i + 1))
                    for half in range(2):
                        dve.bn_stats(stats[:, u, half, :], x_in[:, u, half * 512:(half + 1) * 512]) \
                            .then_inc(stats_done, 1)
                    dve.wait_ge(stats_done, 4 * i + 2 * u + 2)
                    dve.sem_inc(stats_seen, 1)
                    dve.bn_aggr(mv[:, u, :], stats[:, u, :, :]).then_inc(mean_done, 1)
                    dve.wait_ge(mean_done, 2 * i + u + 1)
                    dve.tensor_scalar(mv[:, u, 1:2], mv[:, u, 1:2], EPS, None, ALU.add).then_inc(var_ready, 1)
                for u in range(2):
                    dve.wait_ge(std_ready, 2 * i + u + 1)
                    dve.reciprocal(std[:, u, 1:2], std[:, u, 0:1]).then_inc(rstd_done, 1)
                    dve.wait_ge(rstd_done, 2 * i + u + 1)
                    wait(dve, xt_ready, 2 * i + u - 1)
                    dve.tensor_scalar(xn[:, u, :], x_in[:, u, :], mv[:, u, 0:1], std[:, u, 1:2],
                                      ALU.subtract, ALU.mult).then_inc(xn_ready, 1)
                for u in range(2):
                    dve.wait_ge(xhi_done, 2 * i + u + 1)
                    tok = bass.ds((2 * i + u) * P, P)
                    src = ps[:, 4 + 2 * u:6 + 2 * u, :].rearrange("p b (k n) -> p (b k) n", n=P)
                    dve.tensor_tensor(xlo[:, :, tok], src, xhi[:, :, tok].bitcast(F32), ALU.subtract) \
                        .then_inc(xlo_done, 1)

            normalise(0)
            with dve.Fori(1, TT // 2) as i:
                normalise(i)

            for nb in range(QB):
                dve.wait_ge(mm_ready, quarter(0, nb))
                dve.tensor_copy(qr_t[:, nb * NQ:(nb + 1) * NQ], ps[0:ROUTER, nb, :]).then_inc(lo_done, 1)

            steps = [0]

            def done(ins):
                steps[0] += 1
                ins.then_inc(top_step, 1)

            def before():
                dve.wait_ge(top_step, steps[0])

            dve.wait_ge(score_ready, 1)
            done(dve.tensor_copy(sc_flat, ps[:, 6:8, :].rearrange("p b n -> p (b n)")))
            before()
            for t in range(TT):
                done(dve.max(top[:, t, 0:8], sc[:, t, :]))
            before()
            for t in range(TT):
                done(dve.match_replace(left[:, t, :], top[:, t, 0:8], sc[:, t, :], LOWEST))
            before()
            for t in range(TT):
                done(dve.max(top[:, t, 8:16], left[:, t, :]))
            before()
            for t in range(TT):
                done(dve.match_replace(left[:, t, :], top[:, t, 8:16], left[:, t, :], LOWEST))
            before()
            done(dve.tensor_tensor(left_flat, left_flat, sc_flat, ALU.not_equal))
            before()
            dve.tensor_tensor(sc, sc, top[:, :, 0:1].broadcast_to([P, TT, EXPERTS]), ALU.subtract) \
                .then_inc(shifted_ready, 1)
            dve.wait_ge(gexp_ready, 1)
            done(dve.tensor_tensor(sc_flat, sc_flat, left_flat, ALU.mult))
            before()
            done(dve.tensor_reduce(gsum[:, :, 0:1], sc, AX_X, ALU.add))
            before()
            done(dve.reciprocal(gsum[:, :, 1:2], gsum[:, :, 0:1]))
            before()
            done(dve.tensor_scalar(gsum[:, :, 0:1], gsum[:, :, 1:2], SCALING, None, ALU.mult))
            before()
            dve.tensor_tensor(sc, sc, gsum[:, :, 0:1].broadcast_to([P, TT, EXPERTS]), ALU.mult) \
                .then_inc(gate_ready, 1)

            def rest(i):
                for u, blk in pair(i):
                    wait(dve, stored[u], 32 * i)
                    for nb in range(QB):
                        c = slice(nb * NQ, (nb + 1) * NQ)
                        dve.wait_ge(hi_done, hi_count(blk, nb))
                        dve.scalar_tensor_tensor(out=elo[:, u, c].bitcast(F32R), in0=ps[:, nb, :],
                                                 scalar=wraw[:, (u + 1) % 2, KT * P:WROW], in1=ehi[:, u, c],
                                                 op0=ALU.add, op1=ALU.subtract).then_inc(lo_done, 1)

            rest(0)
            dve.wait_ge(gtr_ready, 1)
            dve.tensor_copy(gate_t, ps[0:EXPERTS, 4:8, :].rearrange("p b n -> p (b n)")).then_inc(gate_t_ready, 1)
            with dve.Fori(1, QK_BLOCKS // 2) as i:
                rest(i)
            with dve.Fori(QK_BLOCKS // 2, (QK_BLOCKS + V_BLOCKS) // 2) as i:
                for u, blk in pair(i):
                    dve.wait_ge(stored[u], 32 * i)
                    for nb in range(QB):
                        dve.wait_ge(vtr_ready, quarter(blk - V0, nb))
                        dve.tensor_copy(elo[:, u, nb * NQ:(nb + 1) * NQ], ps[:, 4 + nb % 2, :]).then_inc(lo_done, 1)
            for b in range(Z_BLOCKS):
                blk, u = Z0 + b, b % 2
                dve.wait_ge(stored[u], 32 * ((blk - 1) // 2))
                dve.wait_ge(gates_loaded[u], 16 * RANK * (b // 2 + 1))
                for nb in range(QB):
                    c = slice(nb * NQ, (nb + 1) * NQ)
                    dve.wait_ge(mm_ready, quarter(blk, nb))
                    dve.tensor_tensor(elo[:, u, c], ps[:, nb, :], gates[:, u, c], ALU.mult).then_inc(lo_done, 1)


def attend(nc, qk_scr, v_scr, recip_scr, cz_scr):
    with ExitStack() as ctx:
        def sb(name, shape, dt=F32):
            return ctx.enter_context(nc.sbuf_tensor(name, shape, dt))

        def sem(name):
            return ctx.enter_context(nc.semaphore(name))

        kp = [sb(f"kp{s}", [P, T], F32R) for s in range(SLOTS)]
        qp = [sb(f"qp{s}", [P, T], F32R) for s in range(SLOTS)]
        vh = [sb(f"vh{s}", [P, TT, HD]) for s in range(SLOTS)]
        probs = [sb(f"probs{s}", [P, T]) for s in range(RING)]
        psum_d = sb("psum_d", [P, T])
        psum_p = [sb(f"psum_p{s}", [P, T]) for s in range(2)]
        raw_ctx = [sb(f"raw_ctx{s}", [P, NQ]) for s in range(2)]
        out_ctx = [sb(f"out_ctx{s}", [P, NQ]) for s in range(2)]
        sums_b = sb("sums_b", [P, NQ])
        sums_q = sb("sums_q", [P, T // P])
        recip_q = sb("recip_q", [P, T // P])
        recip_b = sb("recip_b", [P, NQ])
        part_max = [sb(f"part_max{s}", [P, TT, QB]) for s in range(2)]
        row_max = [sb(f"row_max{s}", [P, TT]) for s in range(2)]
        neg_max = [sb(f"neg_max{s}", [TT, P]) for s in range(SLOTS)]
        ones = sb("ones", [P, HD])
        ident = sb("ident_b", [P, P])
        ps = ctx.enter_context(nc.psum_tensor("ps_b", [P, 8, NQ], F32))
        ST_BANKS, MAX_BANKS = 2, 4
        MAX_BANK, PV_BANK, SUM_BANK = 2, 6, 7

        ident_done = sem("b_ident_done")
        ones_done = sem("ones_done")
        kq_loaded = [sem(f"kq_loaded{s}") for s in range(SLOTS)]
        v_loaded = [sem(f"v_loaded{s}") for s in range(SLOTS)]
        negmax_loaded = [sem(f"negmax_loaded{s}") for s in range(SLOTS)]
        st_ready = sem("st_ready")
        exp_done = sem("exp_done")
        pv_done = sem("pv_done")
        pool_done = sem("pool_done")
        added = sem("added")
        mx_ready = sem("mx_ready")
        mx_free = sem("mx_free")
        rowmax_ready = sem("rowmax_ready")
        raw_done = sem("raw_done")
        sum_ready = sem("sum_ready")
        sums_taken = sem("sums_taken")
        sums_spread = sem("sums_spread")
        recip_done = sem("recip_done")
        recip_stored = sem("recip_stored")
        recip_loaded = sem("recip_loaded")
        ctx_ready = sem("ctx_ready")
        ctx_stored = [sem("ctx_stored0"), sem("ctx_stored1")]

        PROLOGUE = (-1, 2)

        def head(g, j, ahead=0):
            return g + (j + ahead) // SLOTS, (j + ahead) % SLOTS

        def number(g, j):
            return SLOTS * g + j

        def unit(g, j, t, b):
            if (j, isinstance(g, int) and g) == (PROLOGUE[1], PROLOGUE[0]):
                return 4 * t + b, (4 * t + b) % MAX_BANKS
            r = 4 * t + b + (1 if t >= 2 else 0)
            return 4 * 65 * g + 65 * j + 129 + r, (65 * j + 129 + r) % MAX_BANKS

        def transposed_unit(g, j):
            r = 0 if isinstance(g, int) and number(g, j) == HEADS - 2 else 8
            return 4 * 65 * g + 65 * j + 129 + r, (65 * j + 129 + r) % MAX_BANKS

        def pool_count(g, j, t):
            return POOL_OPS * number(g, j) + max(1, POOL_TILES.index(t))

        def added_count(g, j, t):
            return DVE_OPS * number(g, j) + 2 * max(1, DVE_TILES.index(t))

        def scheduled(body):
            body(-1, 2, False, False, True, False)
            body(-1, 3, False, False, True, True)
            for j in range(SLOTS):
                body(0, j, True, j > 0, True, True)

        block = ctx.enter_context(nc.Block())

        @block.sync
        def _(sp):
            def load(g, j):
                h = number(g, j)
                q_row, k_row = h * HD, h * HD + D
                for r, hl in enumerate((0, 1, 0)):
                    sp.dma_start(kp[j][r * HD:(r + 1) * HD, :].bitcast(F32), qk_scr[hl, bass.ds(k_row, HD), :]) \
                        .then_inc(kq_loaded[j], 16)
                for r, hl in enumerate((0, 0, 1)):
                    sp.dma_start(qp[j][r * HD:(r + 1) * HD, :].bitcast(F32), qk_scr[hl, bass.ds(q_row, HD), :]) \
                        .then_inc(kq_loaded[j], 16)
                src = v_scr[bass.ds(g, 1), :, :].rearrange("a p (t c) -> (a p) t c", c=P)[:, :, j * HD:(j + 1) * HD]
                sp.dma_start(vh[j][:, :, :], src).then_inc(v_loaded[j], 16)

            def load_negmax(g, j):
                n, _ = transposed_unit(*head(g, j, -1))
                sp.wait_ge(mx_free, n + 1)
                sp.dma_start(qp[j][PACK:PACK + 1, :].bitcast(F32), neg_max[j][:, :]).then_inc(negmax_loaded[j], 16)

            def invert_sums(g, j):
                h = number(g, j)
                sp.wait_ge(sums_taken, h + 1)
                for b in range(QB):
                    sp.dma_start(sums_q[b * HD:(b + 1) * HD, :], sums_b[b * HD:b * HD + 1, :]) \
                        .then_inc(sums_spread, 16)
                sp.wait_ge(recip_done, h + 1)
                sp.dma_start(recip_scr.rearrange("(p c) -> p c", p=P), recip_q[:, :]).then_inc(recip_stored, 16)
                sp.wait_ge(recip_stored, 16 * (h + 1))
                for b in range(QB):
                    sp.dma_start(recip_b[b * HD:(b + 1) * HD, :],
                                 recip_scr[b * NQ:(b + 1) * NQ].partition_broadcast(HD)).then_inc(recip_loaded, 16)

            def store_ctx(g, j):
                h = number(g, j)
                sp.wait_ge(ctx_ready, h + 1)
                for b in range(QB):
                    sp.dma_start(cz_scr[bass.ds(h * HD, HD), b * NQ:(b + 1) * NQ],
                                 out_ctx[j % 2][b * HD:(b + 1) * HD, :]).then_inc(ctx_stored[j % 2], 16)

            for j in range(SLOTS):
                load(0, j)

            def period(g, j, loads=True, negmax=True, before=True):
                if before:
                    gb, jb = head(g, j, -1)
                    sp.wait_ge(pv_done, 16 * number(g, j))
                    if loads:
                        load(gb + 1, jb)
                if negmax:
                    load_negmax(*head(g, j, 1))
                if before:
                    invert_sums(gb, jb)
                    store_ctx(gb, jb)

            period(-1, 3, before=False)
            for j in range(SLOTS):
                period(0, j, before=j > 0)
            with sp.Fori(1, 7) as g:
                for j in range(SLOTS):
                    period(g, j)
            for j in range(SLOTS):
                period(7, j, loads=j == 0, negmax=j < 3)
            invert_sums(7, 3)
            store_ctx(7, 3)
            for s in range(2):
                sp.wait_ge(ctx_stored[s], 16 * QB * HEADS // 2)

        @block.gpsimd
        def _(pool):
            pool.memset(ident[:, :], 0.0).then_inc(ident_done, 1)
            pool.wait_ge(ident_done, 1)
            pool.affine_select(out=ident[:, :], in_=ident[:, :], compare_op=ALU.not_equal, fill=1.0,
                               base=0, pattern=[[-1, P]], channel_multiplier=1).then_inc(ident_done, 1)
            pool.memset(ones[:, :], 1.0).then_inc(ones_done, 1)
            for s in range(SLOTS):
                pool.wait_ge(ones_done, s + 1)
                pool.memset(kp[s][PACK:PACK + 1, :].bitcast(F32), 1.0).then_inc(ones_done, 1)

            pool.wait_ge(ones_done, SLOTS + 1)

            def period(g, j):
                h = number(g, j)
                acc = psum_p[j % 2]
                wait(pool, sum_ready, h - 1)
                for n, t in enumerate(POOL_TILES[1:]):
                    pool.wait_ge(exp_done, 64 * h + 4 * t + 4)
                    if n:
                        pool.wait_ge(pool_done, pool_count(g, j, POOL_TILES[n]))
                    pool.tensor_tensor(acc[:, :], (acc if n else probs[0])[:, :], probs[t % RING][:, :], ALU.add) \
                        .then_inc(pool_done, 1)
                pool.wait_ge(added, DVE_OPS * (h + 1))
                pool.wait_ge(pool_done, pool_count(g, j, POOL_TILES[-1]))
                pool.tensor_tensor(acc[:, :], acc[:, :], psum_d[:, :], ALU.add).then_inc(pool_done, 1)

            for j in range(SLOTS):
                period(0, j)
            with pool.Fori(1, HEADS // SLOTS) as g:
                for j in range(SLOTS):
                    period(g, j)

        @block.tensor
        def _(pe):
            pe.wait_ge(ident_done, 2)
            pe.wait_ge(ones_done, 1 + SLOTS)

            def scores_t(g, j, t, b):
                h = number(g, j)
                wait(pe, exp_done, 64 * h + 4 * t + b - ST_BANKS + 1)
                pe.matmul(ps[:, b % ST_BANKS, :], kp[j][0:PACK + 1, t * P:(t + 1) * P],
                          qp[j][0:PACK + 1, b * NQ:(b + 1) * NQ], start=True, stop=True).then_inc(st_ready, 1)

            def scores(g, j, t, b):
                gn, jn = head(g, j, 2)
                n, bank = unit(g, j, t, b)
                wait(pe, mx_free, n - MAX_BANKS + 1)
                pe.matmul(ps[:, MAX_BANK + bank, :], qp[jn][0:PACK, t * P:(t + 1) * P],
                          kp[jn][0:PACK, b * NQ:(b + 1) * NQ], start=True, stop=True).then_inc(mx_ready, 1)

            def transpose_max(g, j):
                gn, jn = head(g, j, 1)
                n, bank = transposed_unit(g, j)
                pe.wait_ge(rowmax_ready, number(gn, jn) + 1)
                pe.wait_ge(mx_free, n - MAX_BANKS + 1)
                pe.transpose(ps[0:TT, MAX_BANK + bank, 0:P], row_max[jn % 2][:, :], ident[:, :]).then_inc(mx_ready, 1)

            def values(g, j, t):
                h = number(g, j)
                pe.wait_ge(exp_done, 64 * h + 4 * t + 4)
                if t == 0:
                    pe.wait_ge(v_loaded[j], 16 * (g + 1))
                    wait(pe, raw_done, h)
                for b in range(QB):
                    last = pe.matmul(ps[b * HD:(b + 1) * HD, PV_BANK, :], vh[j][:, t, :],
                                     probs[t % RING][:, b * NQ:(b + 1) * NQ], start=(t == 0), stop=(t == TT - 1))
                if t not in PE_TILES:
                    last.then_inc(pv_done, 1)

            def sums(g, j, t):
                if t not in PE_TILES:
                    return
                if t == PE_TILES[0]:
                    wait(pe, sums_taken, number(g, j))
                for b in range(QB):
                    last = pe.matmul(ps[b * HD:(b + 1) * HD, SUM_BANK, :], ones[:, :],
                                     probs[t % RING][:, b * NQ:(b + 1) * NQ], start=(t == PE_TILES[0]), stop=False)
                last.then_inc(pv_done, 1)

            def pool_sums(g, j):
                h = number(g, j)
                pe.wait_ge(pool_done, POOL_OPS * (h + 1))
                for b in range(QB):
                    last = pe.matmul(ps[b * HD:(b + 1) * HD, SUM_BANK, :], ones[:, :],
                                     psum_p[j % 2][:, b * NQ:(b + 1) * NQ], start=False, stop=True)
                last.then_inc(sum_ready, 1)

            def period(g, j, attends, has_before, maxima, transposes):
                gb, jb = head(g, j, -1)
                gn, jn = head(g, j, 2)
                if attends:
                    pe.wait_ge(negmax_loaded[j], 16 * (g + 1))
                if maxima:
                    pe.wait_ge(kq_loaded[jn], 16 * 6 * (gn + 1))
                for t in range(TT):
                    late = (gb, jb, TT - 1) if t == 0 else (g, j, t - 1)
                    has_late = has_before if t == 0 else attends
                    for half in range(2):
                        for own, b in ((False, 0), (True, 0), (False, 1), (True, 1)) if half == 0 else \
                                ((True, 2), (False, 2), (True, 3), (False, 3)):
                            if own and attends:
                                scores_t(g, j, t, b)
                            if not own and maxima:
                                scores(g, j, t, b)
                        if half == 0 and has_late:
                            values(*late)
                        if half == 1 and has_late:
                            sums(*late)
                        if half == 1 and t == 2 and has_before:
                            pool_sums(gb, jb)
                    if t == 1 and transposes:
                        transpose_max(g, j)

            scheduled(period)
            with pe.Fori(1, 7) as g:
                for j in range(SLOTS):
                    period(g, j, True, True, True, True)
            for j in range(SLOTS):
                period(7, j, True, True, j < 2, j < 3)
            values(7, 3, TT - 1)
            sums(7, 3, TT - 1)
            pool_sums(7, 3)

        @block.scalar
        def _(act):
            def take_raw(g, j):
                h = number(g, j)
                act.wait_ge(pv_done, 16 * (h + 1))
                wait(act, ctx_ready, h - 1)
                act.activation(raw_ctx[j % 2][:, :], ps[:, PV_BANK, :], ACT.Copy).then_inc(raw_done, 1)

            def take_sums(g, j):
                h = number(g, j)
                act.wait_ge(sum_ready, h + 1)
                wait(act, sums_spread, 16 * QB * h)
                act.activation(sums_b[:, :], ps[:, SUM_BANK, :], ACT.Copy).then_inc(sums_taken, 1)

            def period(g, j, has_before=True):
                h = number(g, j)
                for t in range(TT):
                    gr, jr = (g, j) if t >= RING else head(g, j, -1)
                    tr = (t - RING) % TT
                    if has_before or t >= RING:
                        act.wait_ge(pv_done, 16 * h + t - RING + 1)
                        if tr in POOL_TILES:
                            act.wait_ge(pool_done, pool_count(gr, jr, tr))
                        if tr in DVE_TILES:
                            act.wait_ge(added, added_count(gr, jr, tr))
                    for b in range(QB):
                        act.wait_ge(st_ready, 64 * h + 4 * t + b + 1)
                        act.activation(probs[t % RING][:, b * NQ:(b + 1) * NQ], ps[:, b % ST_BANKS, :],
                                       ACT.Exp, scale=SCALE).then_inc(exp_done, 1)
                        if t == 0 and b == 3 and has_before:
                            take_raw(*head(g, j, -1))
                        if t == 3 and b == 3 and has_before:
                            take_sums(*head(g, j, -1))

            for j in range(SLOTS):
                period(0, j, j > 0)
            with act.Fori(1, HEADS // SLOTS) as g:
                for j in range(SLOTS):
                    period(g, j)
            take_raw(7, 3)
            take_sums(7, 3)

        @block.vector
        def _(dve):
            def take_max(g, j, t, b):
                gn, jn = head(g, j, 2)
                n, bank = unit(g, j, t, b)
                dve.wait_ge(mx_ready, n + 1)
                dve.tensor_reduce(part_max[jn % 2][:, t, b:b + 1], ps[:, MAX_BANK + bank, :], AX_X, ALU.max) \
                    .then_inc(mx_free, 1)

            def take_transposed(g, j):
                gn, jn = head(g, j, 1)
                n, bank = transposed_unit(g, j)
                wait(dve, negmax_loaded[jn], 16 * gn)
                dve.wait_ge(mx_ready, n + 1)
                dve.tensor_scalar(neg_max[jn][:, :].bitcast(F32R), ps[0:TT, MAX_BANK + bank, 0:P], -1.0, None,
                                  ALU.mult).then_inc(mx_free, 1)

            def reciprocal(g, j):
                h = number(g, j)
                dve.wait_ge(sums_spread, 16 * QB * (h + 1))
                wait(dve, recip_stored, 16 * h)
                dve.reciprocal(recip_q[:, :], sums_q[:, :]).then_inc(recip_done, 1)

            def add_tile(g, j, n, half):
                h = number(g, j)
                c = slice(half * T // 2, (half + 1) * T // 2)
                a, b = DVE_TILES[n], DVE_TILES[n + 1]
                dve.wait_ge(exp_done, 64 * h + 4 * b + 4)
                if n:
                    dve.wait_ge(added, DVE_OPS * h + 2 * (n - 1) + half + 1)
                else:
                    wait(dve, pool_done, POOL_OPS * h)
                dve.tensor_tensor(psum_d[:, c], (psum_d if n else probs[a % RING])[:, c],
                                  probs[b % RING][:, c], ALU.add).then_inc(added, 1)

            def normalise(g, j):
                h = number(g, j)
                dve.wait_ge(raw_done, h + 1)
                dve.wait_ge(recip_loaded, 16 * QB * (h + 1))
                wait(dve, ctx_stored[j % 2], 16 * QB * (2 * g + j // 2))
                dve.tensor_tensor(out_ctx[j % 2][:, :], raw_ctx[j % 2][:, :], recip_b[:, :], ALU.mult) \
                    .then_inc(ctx_ready, 1)

            def period(g, j, attends, has_before, maxima, transposes):
                gn, jn = head(g, j, 2)
                for t in range(TT):
                    if maxima:
                        for b in range(QB):
                            take_max(g, j, t, b)
                            if t in ADD_AT and b == 0 and attends:
                                add_tile(g, j, *divmod(ADD_AT.index(t), 2))
                    if not maxima and t in ADD_AT:
                        add_tile(g, j, *divmod(ADD_AT.index(t), 2))
                    if t == 1 and transposes:
                        take_transposed(g, j)
                    if t == RECIPROCAL_AT and has_before:
                        reciprocal(*head(g, j, -1))
                    if t == NORMALISE_AT and has_before:
                        normalise(*head(g, j, -1))
                if maxima:
                    n, _ = unit(g, j, TT - 1, QB - 1)
                    dve.wait_ge(mx_free, n + 1)
                    dve.tensor_reduce(row_max[jn % 2][:, :], part_max[jn % 2][:, :, :], AX_X, ALU.max) \
                        .then_inc(rowmax_ready, 1)

            scheduled(period)
            with dve.Fori(1, 7) as g:
                for j in range(SLOTS):
                    period(g, j, True, True, True, True)
            for j in range(SLOTS):
                period(7, j, True, True, j < 2, j < 3)
            reciprocal(7, 3)
            normalise(7, 3)


def project_output(nc, x, w2, bias, cz_scr, out):
    with ExitStack() as ctx:
        def sb(name, shape, dt=F32):
            return ctx.enter_context(nc.sbuf_tensor(name, shape, dt))

        def sem(name):
            return ctx.enter_context(nc.semaphore(name))

        whi = sb("w2hi", [P, OUT_KT, D], F32R)
        wlo = sb("w2lo", [P, OUT_KT, D], F32R)
        wraw = sb("w2raw", [P, 2, D])
        craw = sb("craw", [P, 2, OUT_KT, P])
        chi = sb("chi", [P, 2, OUT_KT, P], F32R)
        clo = sb("clo", [P, 2, OUT_KT, P], F32R)
        xt = sb("xt", [P, 2, D])
        ob = sb("ob", [P, D])
        res = sb("res", [P, 2, D])
        ps = ctx.enter_context(nc.psum_tensor("ps_c", [P, 8, NQ], F32))

        w_loaded = [sem("w2_loaded0"), sem("w2_loaded1")]
        whi_done = sem("w2hi_done")
        wlo_done = sem("w2lo_done")
        c_loaded = [sem("c_loaded0"), sem("c_loaded1")]
        x_loaded = [sem("xc_loaded0"), sem("xc_loaded1")]
        ob_loaded = sem("ob_loaded")
        chi_done = sem("chi_done")
        clo_done = sem("clo_done")
        xb_done = sem("xb_done")
        mm_ready = sem("c_mm_ready")
        res_ready = sem("res_ready")
        out_stored = [sem("out_stored0"), sem("out_stored1")]
        block = ctx.enter_context(nc.Block())

        @block.sync
        def _(sp):
            def load(i, u):
                tok = bass.ds((2 * i + u) * P, P)
                sp.dma_start(craw[:, u, :, :], cz_scr[:, tok].rearrange("(k p) t -> p k t", p=P)) \
                    .then_inc(c_loaded[u], 16)
                sp.dma_start(xt[:, u, :], x[tok, :]).then_inc(x_loaded[u], 16)

            for k in range(2):
                sp.dma_start(wraw[:, k, :], w2[k * P:(k + 1) * P, :]).then_inc(w_loaded[k], 16)
            sp.dma_start(ob[:, :], bias.partition_broadcast(P)).then_inc(ob_loaded, 16)
            for u in range(2):
                load(0, u)
            for k in range(2, OUT_KT):
                sp.wait_ge(wlo_done, k - 1)
                sp.dma_start(wraw[:, k % 2, :], w2[k * P:(k + 1) * P, :]).then_inc(w_loaded[k % 2], 16)
            with sp.Fori(0, TT // 2 - 1) as i:
                for u in range(2):
                    n = 2 * i + u + 1
                    sp.wait_ge(clo_done, n)
                    sp.wait_ge(res_ready, n)
                    load(i + 1, u)
                    sp.dma_start(out[bass.ds((2 * i + u) * P, P), :], res[:, u, :]).then_inc(out_stored[u], 16)
            for u in range(2):
                n = TT - 1 + u
                sp.wait_ge(res_ready, n)
                sp.dma_start(out[(n - 1) * P:n * P, :], res[:, u, :]).then_inc(out_stored[u], 16)
            for u in range(2):
                sp.wait_ge(out_stored[u], 16 * TT // 2)

        @block.gpsimd
        def _(pool):
            pool.wait_ge(ob_loaded, 16)
            with pool.Fori(0, TT // 2) as i:
                for u in range(2):
                    pool.wait_ge(x_loaded[u], 16 * (i + 1))
                    pool.tensor_tensor(xt[:, u, :], xt[:, u, :], ob[:, :], ALU.add).then_inc(xb_done, 1)

        @block.tensor
        def _(pe):
            def tile(i, u, first=False):
                pe.wait_ge(chi_done, 2 * i + u + 1)
                pe.wait_ge(clo_done, 2 * i + u + 1)
                wait(pe, res_ready, 2 * i + u - 1)
                n = 0
                for k in range(OUT_KT):
                    if first:
                        pe.wait_ge(whi_done, k + 1)
                        pe.wait_ge(wlo_done, k + 1)
                    for c, w in ((chi, whi), (chi, wlo), (clo, whi)):
                        for b in range(2):
                            last = pe.matmul(ps[:, 2 * u + b, :], c[:, u, k, :], w[:, k, b * NQ:(b + 1) * NQ],
                                             start=(n == 0), stop=(n == 3 * OUT_KT - 1))
                        n += 1
                last.then_inc(mm_ready, 1)

            tile(0, 0, True)
            tile(0, 1)
            with pe.Fori(1, TT // 2) as i:
                for u in range(2):
                    tile(i, u)

        @block.scalar
        def _(act):
            def split(i, u):
                act.wait_ge(c_loaded[u], 16 * (i + 1))
                wait(act, mm_ready, 2 * i + u - 1)
                act.activation(chi[:, u, :, :], craw[:, u, :, :], ACT.Copy).then_inc(chi_done, 1)

            def split_w(k):
                act.wait_ge(w_loaded[k % 2], 16 * (k // 2 + 1))
                act.activation(whi[:, k, :], wraw[:, k % 2, :], ACT.Copy).then_inc(whi_done, 1)

            split_w(0)
            split_w(1)
            for u in range(2):
                split(0, u)
            for k in range(2, OUT_KT):
                split_w(k)
            with act.Fori(1, TT // 2) as i:
                for u in range(2):
                    split(i, u)

        @block.vector
        def _(dve):
            def split(i, u):
                dve.wait_ge(chi_done, 2 * i + u + 1)
                dve.tensor_tensor(clo[:, u, :, :], craw[:, u, :, :], chi[:, u, :, :].bitcast(F32), ALU.subtract) \
                    .then_inc(clo_done, 1)

            def split_w(k):
                dve.wait_ge(whi_done, k + 1)
                dve.tensor_tensor(wlo[:, k, :], wraw[:, k % 2, :], whi[:, k, :].bitcast(F32), ALU.subtract) \
                    .then_inc(wlo_done, 1)

            def finish(i, u):
                dve.wait_ge(mm_ready, 2 * i + u + 1)
                dve.wait_ge(xb_done, 2 * i + u + 1)
                wait(dve, out_stored[u], 16 * i)
                dve.tensor_tensor(res[:, u, :], ps[:, 2 * u:2 * u + 2, :].rearrange("p b n -> p (b n)"),
                                  xt[:, u, :], ALU.add).then_inc(res_ready, 1)

            split_w(0)
            split_w(1)
            for u in range(2):
                split(0, u)
            for k in range(2, OUT_KT):
                split_w(k)
            for u in range(2):
                finish(0, u)
                split(1, u)
            with dve.Fori(1, TT // 2 - 1) as i:
                for u in range(2):
                    finish(i, u)
                    split(i + 1, u)
            for u in range(2):
                finish(TT // 2 - 1, u)


def build(nc, x, wcat, keys_t, w2, bias, out):
    qk_scr = nc.dram_tensor("qk_scr", [2, 2 * D, T], F32, kind="Internal").ap()
    v_scr = nc.dram_tensor("v_scr", [V_BLOCKS, P, T], F32, kind="Internal").ap()
    gate_scr = nc.dram_tensor("gate_scr", [EXPERTS, T], F32, kind="Internal").ap()
    recip_scr = nc.dram_tensor("recip_scr", [T], F32, kind="Internal").ap()
    cz_scr = nc.dram_tensor("cz_scr", [D + BOTTLENECK, T], F32, kind="Internal").ap()
    project_inputs(nc, x, wcat, keys_t, qk_scr, v_scr, gate_scr, cz_scr)
    attend(nc, qk_scr, v_scr, recip_scr, cz_scr)
    project_output(nc, x, w2, bias, cz_scr, out)


def kernel(**inputs):
    import numpy as np
    import concourse.bacc as bacc
    from concourse.bass_utils import run_bass_kernel_spmd

    x = np.ascontiguousarray(inputs["L0_attn_x"]).reshape(T, D)
    qkvw = np.asarray(inputs["L0_attn_attn_qkvw"])
    qkvb = np.asarray(inputs["L0_attn_attn_qkvb"])
    router = np.zeros((D, P), np.float32)
    router[:, :ROUTER] = np.asarray(inputs["L0_ffn_Wq_w"]).T
    cols = np.concatenate([router, qkvw, np.asarray(inputs["L0_ffn_A_w"]).T], axis=1)
    wcat = np.zeros((BLOCKS, P, WROW), np.float32)
    wcat[:, :, :KT * P] = cols.reshape(KT, P, BLOCKS, P).transpose(2, 1, 0, 3).reshape(BLOCKS, P, KT * P)
    wcat[1:Z0, :, KT * P] = qkvb.reshape(Z0 - 1, P)
    arrays = {
        "x": x,
        "wcat": wcat,
        "keys_t": np.ascontiguousarray(np.asarray(inputs["L0_ffn_keys"]).T),
        "w2": np.concatenate([np.asarray(inputs["L0_attn_attn_ow"]), np.asarray(inputs["L0_ffn_B_w"]).T], axis=0),
        "bias": np.ascontiguousarray(inputs["L0_attn_attn_ob"]),
    }
    nc = bacc.Bacc("TRN2", target_bir_lowering=False, num_devices=1)
    aps = [nc.dram_tensor(n, a.shape, F32, kind="ExternalInput").ap() for n, a in arrays.items()]
    out = nc.dram_tensor("out", [T, D], F32, kind="ExternalOutput").ap()
    build(nc, *aps, out)
    r = run_bass_kernel_spmd(nc, [arrays], core_ids=[0])
    return r.results[0]["out"].reshape(1, T, D)
```

```python
from contextlib import ExitStack

import concourse.bass as bass
from concourse import mybir

F32 = mybir.dt.float32
F32R = mybir.dt.float32r
ALU = mybir.AluOpType
ACT = mybir.ActivationFunctionType
AX_X = mybir.AxisListType.X

P = 128
T = 2048
D = 1024
HEADS = 32
HD = D // HEADS
SCALE = HD ** -0.5
EPS = 1e-5
KT = D // P
TT = T // P
NQ = 512
QB = T // NQ
CHUNK = NQ // P
EXPERTS = 64
RANK = 8
BOTTLENECK = EXPERTS * RANK
ROUTER = 16
SCALING = 2.0
LOWEST = -3.0e38

ROUTER_BLOCK = 0
QK_BLOCKS = 2 * D // P
V_BLOCKS = D // P
Z_BLOCKS = BOTTLENECK // P
V0 = 1 + QK_BLOCKS
Z0 = V0 + V_BLOCKS
BLOCKS = Z0 + Z_BLOCKS
WROW = KT * P + 1

PACK = 3 * HD

POOL_TILES = [0, 1, 2, 4, 6, 7, 8, 10, 11, 12]
DVE_TILES = [3, 5, 9]
PE_TILES = [t for t in range(TT) if t not in POOL_TILES + DVE_TILES]
POOL_OPS = len(POOL_TILES)
DVE_OPS = QB * (len(DVE_TILES) - 1)
RECIPROCAL_AT, NORMALISE_AT = 7, 10
ADD_AT = [6, 7, 8, 9, 10, 11, 12, 13]
RING = 8
SLOTS = 4

OUT_KT = KT + Z_BLOCKS


def wait(eng, sem, value):
    if isinstance(value, int) and value <= 0:
        return
    eng.wait_ge(sem, value)


def project_inputs(nc, x, wcat, keys_t, qk_scr, v_scr, gate_scr, cz_scr):
    with ExitStack() as ctx:
        def sb(name, shape, dt=F32):
            return ctx.enter_context(nc.sbuf_tensor(name, shape, dt))

        def sem(name):
            return ctx.enter_context(nc.semaphore(name))

        xhi = sb("xhi", [P, KT, T], F32R)
        xlo = sb("xlo", [P, KT, T], F32R)
        wraw = sb("wraw", [P, 2, WROW])
        whi = sb("whi", [P, 2, KT * P], F32R)
        wlo = sb("wlo", [P, 2, KT * P], F32R)
        ehi = sb("ehi", [P, 2, T])
        elo = sb("elo", [P, 2, T])
        stage = sb("stage", [P, 2 * T])
        ident = sb("ident", [P, P])
        keys = sb("keys", [ROUTER, EXPERTS])
        stats = sb("stats", [P, CHUNK, 2, 6])
        mv = sb("mv", [P, CHUNK, 2])
        std = sb("std", [P, CHUNK, 2])
        top = sb("top", [P, TT, 16])
        gsum = sb("gsum", [P, TT, 2])
        ps = ctx.enter_context(nc.psum_tensor("ps_a", [P, 8, NQ], F32))
        ps_flat = ps[:, :, :].rearrange("p b n -> p (b n)")

        x_in = stage[:, :].rearrange("p (s d) -> p s d", s=CHUNK)
        xn = ehi[:, :, :].rearrange("p u (v d) -> p (u v) d", v=2)
        qr_t = elo[0:ROUTER, 1, :]
        sc_flat = stage[:, T:T + TT * EXPERTS]
        sc = sc_flat.rearrange("p (t e) -> p t e", e=EXPERTS)
        left_flat = stage[:, T + TT * EXPERTS:T + 2 * TT * EXPERTS]
        left = left_flat.rearrange("p (t e) -> p t e", e=EXPERTS)
        gate_t = stage[0:EXPERTS, 0:T]
        gates = stage[:, :].rearrange("p (u t) -> p u t", u=2)

        x_loaded = [sem(f"x_loaded{i}") for i in range(CHUNK)]
        ident_done = sem("ident_done")
        keys_loaded = sem("keys_loaded")
        stats_done = sem("stats_done")
        stats_seen = sem("stats_seen")
        mean_done = sem("mean_done")
        var_ready = sem("var_ready")
        std_ready = sem("std_ready")
        rstd_done = sem("rstd_done")
        xn_ready = sem("xn_ready")
        xt_ready = sem("xt_ready")
        xhi_done = sem("xhi_done")
        xlo_done = sem("xlo_done")
        w_loaded = [sem("w_loaded0"), sem("w_loaded1")]
        whi_done = sem("whi_done")
        wlo_done = sem("wlo_done")
        mm_ready = sem("mm_ready")
        hi_done = sem("hi_done")
        lo_done = sem("lo_done")
        stored = [sem("stored0"), sem("stored1")]
        score_ready = sem("score_ready")
        top_step = sem("top_step")
        shifted_ready = sem("shifted_ready")
        gexp_ready = sem("gexp_ready")
        gate_ready = sem("gate_ready")
        gtr_ready = sem("gtr_ready")
        gate_t_ready = sem("gate_t_ready")
        gate_stored = sem("gate_stored")
        gates_loaded = [sem("gates_loaded0"), sem("gates_loaded1")]
        vtr_ready = sem("vtr_ready")

        def quarter(blk, nb):
            return 4 * blk + nb + 1

        def product(blk, nb):
            return 2 * nb + blk + 1 if isinstance(blk, int) and blk < 2 else quarter(blk, nb)

        def hi_count(blk, nb):
            return 4 * blk + nb - 3

        def transposed(t):
            u = t % 2
            return ps[:, 4 + 2 * u:6 + 2 * u, :].rearrange("p b (k n) -> p (b k) n", n=P)

        def pair(i):
            return [(u, 2 * i + u + 1) for u in range(2)]

        block = ctx.enter_context(nc.Block())

        @block.sync
        def _(sp):
            def load_w(blk, slot):
                sp.dma_start(wraw[:, slot, :], wcat[bass.ds(blk, 1), :, :].rearrange("a p n -> (a p) n")) \
                    .then_inc(w_loaded[slot], 16)

            def load_gates(b, u):
                for r in range(RANK):
                    sp.dma_start(gates[r::RANK, u, :], gate_scr[16 * b:16 * b + 16, :]) \
                        .then_inc(gates_loaded[u], 16)

            def store_qk(blk, u):
                row = (blk - 1) * P
                for part, ev in ((0, ehi), (1, elo)):
                    sp.dma_start(qk_scr[part, bass.ds(row, P), :], ev[:, u, :]).then_inc(stored[u], 16)

            sp.dma_start(keys[:, :], keys_t).then_inc(keys_loaded, 16)
            load_w(0, 0)
            load_w(1, 1)
            for t in range(CHUNK):
                sp.dma_start(x_in[:, t, :], x[t * P:(t + 1) * P, :]).then_inc(x_loaded[t], 16)
            with sp.Fori(1, QB) as c:
                for t in range(CHUNK):
                    sp.wait_ge(xn_ready, CHUNK * c + t - CHUNK + 1)
                    sp.dma_start(x_in[:, t, :], x[bass.ds((CHUNK * c + t) * P, P), :]).then_inc(x_loaded[t], 16)
            sp.wait_ge(wlo_done, 1)
            load_w(2, 0)

            def after_qk(i):
                for u, blk in pair(i):
                    sp.wait_ge(lo_done, quarter(blk, 3))
                    store_qk(blk, u)
                    load_w(blk + 2, (u + 1) % 2)

            after_qk(0)
            sp.wait_ge(gate_t_ready, 1)
            sp.dma_start(gate_scr, gate_t).then_inc(gate_stored, 16)
            with sp.Fori(1, QK_BLOCKS // 2) as i:
                after_qk(i)
            sp.wait_ge(gate_stored, 16)
            for u in range(2):
                load_gates(u, u)
            with sp.Fori(QK_BLOCKS // 2, (QK_BLOCKS + V_BLOCKS) // 2) as i:
                for u, blk in pair(i):
                    sp.wait_ge(lo_done, quarter(blk, 3))
                    vb = blk - V0
                    for half in range(2):
                        c = slice(half * T // 2, (half + 1) * T // 2)
                        sp.dma_start(v_scr[bass.ds(vb, 1), :, c].rearrange("a p n -> (a p) n"), elo[:, u, c]) \
                            .then_inc(stored[u], 16)
                    load_w(blk + 2, (u + 1) % 2)
            for b in range(Z_BLOCKS):
                blk, u = Z0 + b, b % 2
                sp.wait_ge(lo_done, quarter(blk, 3))
                for half in range(2):
                    c = slice(half * T // 2, (half + 1) * T // 2)
                    sp.dma_start(cz_scr[D + b * P:D + (b + 1) * P, c], elo[:, u, c]).then_inc(stored[u], 16)
                if blk + 2 < BLOCKS:
                    load_w(blk + 2, (u + 1) % 2)
                    load_gates(b + 2, u)
            for u in range(2):
                sp.wait_ge(stored[u], 32 * (BLOCKS - 1) // 2)

        @block.gpsimd
        def _(pool):
            pool.memset(ident[:, :], 0.0).then_inc(ident_done, 1)
            pool.wait_ge(ident_done, 1)
            pool.affine_select(out=ident[:, :], in_=ident[:, :], compare_op=ALU.not_equal, fill=1.0,
                               base=0, pattern=[[-1, P]], channel_multiplier=1).then_inc(ident_done, 1)

            def split(blk, slot):
                pool.wait_ge(whi_done, blk + 1)
                pool.tensor_tensor(wlo[:, slot, :], wraw[:, slot, 0:KT * P], whi[:, slot, :].bitcast(F32),
                                   ALU.subtract).then_inc(wlo_done, 1)

            split(0, 0)
            with pool.Fori(0, (BLOCKS - 1) // 2) as i:
                for u, blk in pair(i):
                    split(blk, (u + 1) % 2)

        @block.tensor
        def _(pe):
            pe.wait_ge(ident_done, 2)

            def transpose_x(c, half):
                for t in (2 * half, 2 * half + 1):
                    n = CHUNK * c + t
                    pe.wait_ge(xn_ready, n + 1)
                    wait(pe, xlo_done, n - 1)
                    for k in range(KT):
                        last = pe.transpose(ps[:, 4 + 2 * (t % 2) + k // 4, (k % 4) * P:(k % 4 + 1) * P],
                                            xn[:, t, k * P:(k + 1) * P], ident[:, :])
                    last.then_inc(xt_ready, 1)

            def project(slot, nb):
                n = 0
                tk = bass.ds(nb * NQ, NQ)
                for k in range(KT):
                    wk = slice(k * P, (k + 1) * P)
                    for w, xx in ((whi, xhi), (whi, xlo), (wlo, xhi)):
                        last = pe.matmul(ps_flat[:, tk], w[:, slot, wk], xx[:, k, tk],
                                         start=(n == 0), stop=(n == 3 * KT - 1))
                        n += 1
                last.then_inc(mm_ready, 1)

            def qk_block(u, blk):
                pe.wait_ge(wlo_done, blk + 1)
                for nb in range(QB):
                    wait(pe, lo_done, quarter(blk - 1, nb))
                    project((u + 1) % 2, nb)

            def first_block(blk, c):
                pe.wait_ge(wlo_done, blk + 1)
                if blk == 0:
                    pe.wait_ge(xhi_done, CHUNK * (c + 1))
                    pe.wait_ge(xlo_done, CHUNK * (c + 1))
                else:
                    pe.wait_ge(lo_done, c + 1)
                project(blk, c)

            for half in range(2):
                transpose_x(0, half)
            with pe.Fori(1, QB) as c:
                for blk in range(2):
                    transpose_x(c, blk)
                    first_block(blk, c - 1)
            for blk in range(2):
                first_block(blk, QB - 1)

            pe.wait_ge(lo_done, quarter(0, 3))
            pe.wait_ge(keys_loaded, 16)
            for t in range(TT):
                last = pe.matmul(ps[:, 6 + t // 8, (t % 8) * EXPERTS:(t % 8 + 1) * EXPERTS],
                                 qr_t[:, t * P:(t + 1) * P], keys[:, :], start=True, stop=True)
            last.then_inc(score_ready, 1)
            qk_block(1, 2)
            pe.wait_ge(gate_ready, 1)
            for t in range(TT):
                last = pe.transpose(ps[0:EXPERTS, 4 + t // 4, (t % 4) * P:(t % 4 + 1) * P], sc[:, t, :], ident[:, :])
            last.then_inc(gtr_ready, 1)
            with pe.Fori(1, QK_BLOCKS // 2) as i:
                for u, blk in pair(i):
                    qk_block(u, blk)
            pe.wait_ge(gate_t_ready, 1)

            def transpose_v(u, blk, nb):
                pe.wait_ge(hi_done, hi_count(blk, nb))
                pe.wait_ge(lo_done, quarter(blk, nb) - 2)
                for t in range(4):
                    c = slice(nb * NQ + t * P, nb * NQ + (t + 1) * P)
                    last = pe.transpose(ps[:, 4 + nb % 2, t * P:(t + 1) * P], ehi[:, u, c], ident[:, :])
                last.then_inc(vtr_ready, 1)

            with pe.Fori(QK_BLOCKS // 2, (QK_BLOCKS + V_BLOCKS) // 2) as i:
                for u, blk in pair(i):
                    pe.wait_ge(wlo_done, blk + 1)
                    for nb in range(QB):
                        pe.wait_ge(lo_done, quarter(V0 - 1, nb))
                        pe.wait_ge(hi_done, hi_count(blk - 1, nb))
                        project((u + 1) % 2, nb)
                        if nb >= 1:
                            transpose_v(u, blk, nb - 1)
                    transpose_v(u, blk, QB - 1)
            for b in range(Z_BLOCKS):
                qk_block(b % 2, Z0 + b)

        @block.scalar
        def _(act):
            def round_w(blk, slot, loads):
                act.wait_ge(w_loaded[slot], 16 * loads)
                wait(act, mm_ready, product(blk - 2, 3) if not isinstance(blk, int) or blk >= 2 else 0)
                act.activation(whi[:, slot, :], wraw[:, slot, 0:KT * P], ACT.Copy).then_inc(whi_done, 1)

            round_w(0, 0, 1)
            round_w(1, 1, 1)

            def deviation(c, half):
                for t in (2 * half, 2 * half + 1):
                    act.wait_ge(var_ready, CHUNK * c + t + 1)
                    act.activation(std[:, t, 0:1], mv[:, t, 1:2], ACT.Sqrt).then_inc(std_ready, 1)

            def round_x(c, half):
                for t in (2 * half, 2 * half + 1):
                    act.wait_ge(xt_ready, CHUNK * c + t + 1)
                    act.activation(xhi[:, :, bass.ds((CHUNK * c + t) * P, P)], transposed(t), ACT.Copy) \
                        .then_inc(xhi_done, 1)

            deviation(0, 0)
            deviation(0, 1)
            round_x(0, 0)
            with act.Fori(1, QB) as c:
                deviation(c, 0)
                round_x(c - 1, 1)
                deviation(c, 1)
                round_x(c, 0)
            round_x(QB - 1, 1)

            def q_part(u, blk, nb, rounded):
                c = slice(nb * NQ, (nb + 1) * NQ)
                act.wait_ge(mm_ready, product(blk, nb))
                dst = ehi[:, u, c].bitcast(F32R) if rounded else ehi[:, u, c]
                act.activation(dst, ps[:, nb, :], ACT.Identity,
                               bias=wraw[:, (u + 1) % 2, KT * P:WROW]).then_inc(hi_done, 1)

            def part(i, rounded):
                for u, blk in pair(i):
                    act.wait_ge(stored[u], 32 * i)
                    for nb in range(QB):
                        if nb == 1:
                            round_w(blk + 1, u, i + 2)
                        q_part(u, blk, nb, rounded)

            for u, blk in pair(0):
                for nb in range(QB):
                    if nb == QB - 1 - 2 * u:
                        round_w(blk + 1, u, 2)
                    q_part(u, blk, nb, True)
                if u == 0:
                    act.wait_ge(shifted_ready, 1)
                    act.activation(sc_flat, sc_flat, ACT.Exp).then_inc(gexp_ready, 1)
            with act.Fori(1, QK_BLOCKS // 2) as i:
                part(i, True)
            with act.Fori(QK_BLOCKS // 2, (QK_BLOCKS + V_BLOCKS) // 2) as i:
                part(i, False)
            for blk in range(Z0 + 1, BLOCKS):
                round_w(blk, blk % 2, blk // 2 + 1)

        @block.vector
        def _(dve):
            def normalise(c, half):
                for t in (2 * half, 2 * half + 1):
                    n = CHUNK * c + t
                    dve.wait_ge(x_loaded[t], 16 * (c + 1))
                    for part in range(2):
                        dve.bn_stats(stats[:, t, part, :], x_in[:, t, part * 512:(part + 1) * 512]) \
                            .then_inc(stats_done, 1)
                    dve.wait_ge(stats_done, 2 * n + 2)
                    dve.sem_inc(stats_seen, 1)
                    dve.bn_aggr(mv[:, t, :], stats[:, t, :, :]).then_inc(mean_done, 1)
                    dve.wait_ge(mean_done, n + 1)
                    dve.tensor_scalar(mv[:, t, 1:2], mv[:, t, 1:2], EPS, None, ALU.add).then_inc(var_ready, 1)
                for t in (2 * half, 2 * half + 1):
                    n = CHUNK * c + t
                    dve.wait_ge(std_ready, n + 1)
                    dve.reciprocal(std[:, t, 1:2], std[:, t, 0:1]).then_inc(rstd_done, 1)
                    dve.wait_ge(rstd_done, n + 1)
                    wait(dve, xt_ready, n - CHUNK + 1)
                    dve.tensor_scalar(xn[:, t, :], x_in[:, t, :], mv[:, t, 0:1], std[:, t, 1:2],
                                      ALU.subtract, ALU.mult).then_inc(xn_ready, 1)

            def rest_x(c, half):
                for t in (2 * half, 2 * half + 1):
                    n = CHUNK * c + t
                    dve.wait_ge(xhi_done, n + 1)
                    tok = bass.ds(n * P, P)
                    dve.tensor_tensor(xlo[:, :, tok], transposed(t), xhi[:, :, tok].bitcast(F32), ALU.subtract) \
                        .then_inc(xlo_done, 1)

            def router_query(c):
                dve.wait_ge(mm_ready, product(0, c))
                tok = bass.ds(c * NQ, NQ)
                dve.tensor_copy(qr_t[:, tok], ps_flat[0:ROUTER, tok]).then_inc(lo_done, 1)

            normalise(0, 0)
            normalise(0, 1)
            rest_x(0, 0)
            with dve.Fori(1, QB) as c:
                normalise(c, 0)
                rest_x(c - 1, 1)
                normalise(c, 1)
                rest_x(c, 0)
                router_query(c - 1)
            rest_x(QB - 1, 1)
            router_query(QB - 1)

            def rest(u, blk):
                for nb in range(QB):
                    c = slice(nb * NQ, (nb + 1) * NQ)
                    dve.wait_ge(hi_done, hi_count(blk, nb))
                    dve.scalar_tensor_tensor(out=elo[:, u, c].bitcast(F32R), in0=ps[:, nb, :],
                                             scalar=wraw[:, (u + 1) % 2, KT * P:WROW], in1=ehi[:, u, c],
                                             op0=ALU.add, op1=ALU.subtract).then_inc(lo_done, 1)

            rest(0, 1)

            steps = [0]

            def done(ins):
                steps[0] += 1
                ins.then_inc(top_step, 1)

            def before():
                dve.wait_ge(top_step, steps[0])

            dve.wait_ge(score_ready, 1)
            done(dve.tensor_copy(sc_flat, ps[:, 6:8, :].rearrange("p b n -> p (b n)")))
            before()
            for t in range(TT):
                done(dve.max(top[:, t, 0:8], sc[:, t, :]))
            before()
            for t in range(TT):
                done(dve.match_replace(left[:, t, :], top[:, t, 0:8], sc[:, t, :], LOWEST))
            before()
            for t in range(TT):
                done(dve.max(top[:, t, 8:16], left[:, t, :]))
            before()
            for t in range(TT):
                done(dve.match_replace(left[:, t, :], top[:, t, 8:16], left[:, t, :], LOWEST))
            before()
            done(dve.tensor_tensor(left_flat, left_flat, sc_flat, ALU.not_equal))
            before()
            dve.tensor_tensor(sc, sc, top[:, :, 0:1].broadcast_to([P, TT, EXPERTS]), ALU.subtract) \
                .then_inc(shifted_ready, 1)
            dve.wait_ge(gexp_ready, 1)
            done(dve.tensor_tensor(sc_flat, sc_flat, left_flat, ALU.mult))
            before()
            done(dve.tensor_reduce(gsum[:, :, 0:1], sc, AX_X, ALU.add))
            before()
            done(dve.reciprocal(gsum[:, :, 1:2], gsum[:, :, 0:1]))
            before()
            done(dve.tensor_scalar(gsum[:, :, 0:1], gsum[:, :, 1:2], SCALING, None, ALU.mult))
            before()
            dve.tensor_tensor(sc, sc, gsum[:, :, 0:1].broadcast_to([P, TT, EXPERTS]), ALU.mult) \
                .then_inc(gate_ready, 1)

            rest(1, 2)
            dve.wait_ge(gtr_ready, 1)
            dve.tensor_copy(gate_t, ps[0:EXPERTS, 4:8, :].rearrange("p b n -> p (b n)")).then_inc(gate_t_ready, 1)
            with dve.Fori(1, QK_BLOCKS // 2) as i:
                for u, blk in pair(i):
                    dve.wait_ge(stored[u], 32 * i)
                    rest(u, blk)
            with dve.Fori(QK_BLOCKS // 2, (QK_BLOCKS + V_BLOCKS) // 2) as i:
                for u, blk in pair(i):
                    dve.wait_ge(stored[u], 32 * i)
                    for nb in range(QB):
                        dve.wait_ge(vtr_ready, quarter(blk - V0, nb))
                        dve.tensor_copy(elo[:, u, nb * NQ:(nb + 1) * NQ], ps[:, 4 + nb % 2, :]).then_inc(lo_done, 1)
            for b in range(Z_BLOCKS):
                blk, u = Z0 + b, b % 2
                dve.wait_ge(stored[u], 32 * ((blk - 1) // 2))
                dve.wait_ge(gates_loaded[u], 16 * RANK * (b // 2 + 1))
                for nb in range(QB):
                    c = slice(nb * NQ, (nb + 1) * NQ)
                    dve.wait_ge(mm_ready, quarter(blk, nb))
                    dve.tensor_tensor(elo[:, u, c], ps[:, nb, :], gates[:, u, c], ALU.mult).then_inc(lo_done, 1)


def attend(nc, qk_scr, v_scr, recip_scr, cz_scr):
    with ExitStack() as ctx:
        def sb(name, shape, dt=F32):
            return ctx.enter_context(nc.sbuf_tensor(name, shape, dt))

        def sem(name):
            return ctx.enter_context(nc.semaphore(name))

        kp = [sb(f"kp{s}", [P, T], F32R) for s in range(SLOTS)]
        qp = [sb(f"qp{s}", [P, T], F32R) for s in range(SLOTS)]
        vh = [sb(f"vh{s}", [P, TT, HD]) for s in range(SLOTS)]
        probs = [sb(f"probs{s}", [P, T]) for s in range(RING)]
        psum_d = sb("psum_d", [P, T])
        psum_p = [sb(f"psum_p{s}", [P, T]) for s in range(2)]
        raw_ctx = [sb(f"raw_ctx{s}", [P, NQ]) for s in range(2)]
        out_ctx = [sb(f"out_ctx{s}", [P, NQ]) for s in range(2)]
        sums_b = sb("sums_b", [P, NQ])
        sums_q = sb("sums_q", [P, T // P])
        recip_q = sb("recip_q", [P, T // P])
        recip_b = sb("recip_b", [P, NQ])
        part_max = [sb(f"part_max{s}", [P, TT, QB]) for s in range(2)]
        row_max = [sb(f"row_max{s}", [P, TT]) for s in range(2)]
        neg_max = [sb(f"neg_max{s}", [TT, P]) for s in range(SLOTS)]
        ones = sb("ones", [P, HD])
        ident = sb("ident_b", [P, P])
        ps = ctx.enter_context(nc.psum_tensor("ps_b", [P, 8, NQ], F32))
        ST_BANKS, MAX_BANKS = 2, 4
        MAX_BANK, PV_BANK, SUM_BANK = 2, 6, 7

        ident_done = sem("b_ident_done")
        ones_done = sem("ones_done")
        kq_loaded = [sem(f"kq_loaded{s}") for s in range(SLOTS)]
        v_loaded = [sem(f"v_loaded{s}") for s in range(SLOTS)]
        negmax_loaded = [sem(f"negmax_loaded{s}") for s in range(SLOTS)]
        st_ready = sem("st_ready")
        exp_done = sem("exp_done")
        pv_done = sem("pv_done")
        pool_done = sem("pool_done")
        added = sem("added")
        mx_ready = sem("mx_ready")
        mx_free = sem("mx_free")
        rowmax_ready = sem("rowmax_ready")
        raw_done = sem("raw_done")
        sum_ready = sem("sum_ready")
        sums_taken = sem("sums_taken")
        sums_spread = sem("sums_spread")
        recip_done = sem("recip_done")
        recip_stored = sem("recip_stored")
        recip_loaded = sem("recip_loaded")
        ctx_ready = sem("ctx_ready")
        ctx_stored = [sem("ctx_stored0"), sem("ctx_stored1")]

        PROLOGUE = (-1, 2)

        def head(g, j, ahead=0):
            return g + (j + ahead) // SLOTS, (j + ahead) % SLOTS

        def number(g, j):
            return SLOTS * g + j

        def unit(g, j, t, b):
            if (j, isinstance(g, int) and g) == (PROLOGUE[1], PROLOGUE[0]):
                return 4 * t + b, (4 * t + b) % MAX_BANKS
            r = 4 * t + b + (1 if t >= 2 else 0)
            return 4 * 65 * g + 65 * j + 129 + r, (65 * j + 129 + r) % MAX_BANKS

        def transposed_unit(g, j):
            r = 0 if isinstance(g, int) and number(g, j) == HEADS - 2 else 8
            return 4 * 65 * g + 65 * j + 129 + r, (65 * j + 129 + r) % MAX_BANKS

        def pool_count(g, j, t):
            return POOL_OPS * number(g, j) + max(1, POOL_TILES.index(t))

        def added_count(g, j, t):
            return DVE_OPS * number(g, j) + QB * max(1, DVE_TILES.index(t))

        def scheduled(body):
            body(-1, 2, False, False, True, False)
            body(-1, 3, False, False, True, True)
            for j in range(SLOTS):
                body(0, j, True, j > 0, True, True)

        block = ctx.enter_context(nc.Block())

        @block.sync
        def _(sp):
            def load(g, j):
                h = number(g, j)
                q_row, k_row = h * HD, h * HD + D
                for r, hl in enumerate((0, 1, 0)):
                    sp.dma_start(kp[j][r * HD:(r + 1) * HD, :].bitcast(F32), qk_scr[hl, bass.ds(k_row, HD), :]) \
                        .then_inc(kq_loaded[j], 16)
                for r, hl in enumerate((0, 0, 1)):
                    sp.dma_start(qp[j][r * HD:(r + 1) * HD, :].bitcast(F32), qk_scr[hl, bass.ds(q_row, HD), :]) \
                        .then_inc(kq_loaded[j], 16)
                src = v_scr[bass.ds(g, 1), :, :].rearrange("a p (t c) -> (a p) t c", c=P)[:, :, j * HD:(j + 1) * HD]
                sp.dma_start(vh[j][:, :, :], src).then_inc(v_loaded[j], 16)

            def load_negmax(g, j):
                n, _ = transposed_unit(*head(g, j, -1))
                sp.wait_ge(mx_free, n + 1)
                sp.dma_start(qp[j][PACK:PACK + 1, :].bitcast(F32), neg_max[j][:, :]).then_inc(negmax_loaded[j], 16)

            def invert_sums(g, j):
                h = number(g, j)
                sp.wait_ge(sums_taken, h + 1)
                for b in range(QB):
                    sp.dma_start(sums_q[b * HD:(b + 1) * HD, :], sums_b[b * HD:b * HD + 1, :]) \
                        .then_inc(sums_spread, 16)
                sp.wait_ge(recip_done, h + 1)
                sp.dma_start(recip_scr.rearrange("(p c) -> p c", p=P), recip_q[:, :]).then_inc(recip_stored, 16)
                sp.wait_ge(recip_stored, 16 * (h + 1))
                for b in range(QB):
                    sp.dma_start(recip_b[b * HD:(b + 1) * HD, :],
                                 recip_scr[b * NQ:(b + 1) * NQ].partition_broadcast(HD)).then_inc(recip_loaded, 16)

            def store_ctx(g, j):
                h = number(g, j)
                sp.wait_ge(ctx_ready, h + 1)
                for b in range(QB):
                    sp.dma_start(cz_scr[bass.ds(h * HD, HD), b * NQ:(b + 1) * NQ],
                                 out_ctx[j % 2][b * HD:(b + 1) * HD, :]).then_inc(ctx_stored[j % 2], 16)

            for j in range(SLOTS):
                load(0, j)

            def period(g, j, loads=True, negmax=True, before=True):
                if before:
                    gb, jb = head(g, j, -1)
                    sp.wait_ge(pv_done, 16 * number(g, j))
                    if loads:
                        load(gb + 1, jb)
                if negmax:
                    load_negmax(*head(g, j, 1))
                if before:
                    invert_sums(gb, jb)
                    store_ctx(gb, jb)

            period(-1, 3, before=False)
            for j in range(SLOTS):
                period(0, j, before=j > 0)
            with sp.Fori(1, 7) as g:
                for j in range(SLOTS):
                    period(g, j)
            for j in range(SLOTS):
                period(7, j, loads=j == 0, negmax=j < 3)
            invert_sums(7, 3)
            store_ctx(7, 3)
            for s in range(2):
                sp.wait_ge(ctx_stored[s], 16 * QB * HEADS // 2)

        @block.gpsimd
        def _(pool):
            pool.memset(ident[:, :], 0.0).then_inc(ident_done, 1)
            pool.wait_ge(ident_done, 1)
            pool.affine_select(out=ident[:, :], in_=ident[:, :], compare_op=ALU.not_equal, fill=1.0,
                               base=0, pattern=[[-1, P]], channel_multiplier=1).then_inc(ident_done, 1)
            pool.memset(ones[:, :], 1.0).then_inc(ones_done, 1)
            for s in range(SLOTS):
                pool.wait_ge(ones_done, s + 1)
                pool.memset(kp[s][PACK:PACK + 1, :].bitcast(F32), 1.0).then_inc(ones_done, 1)

            pool.wait_ge(ones_done, SLOTS + 1)

            def period(g, j):
                h = number(g, j)
                acc = psum_p[j % 2]
                wait(pool, sum_ready, h - 1)
                for n, t in enumerate(POOL_TILES[1:]):
                    pool.wait_ge(exp_done, 64 * h + 4 * t + 4)
                    if n:
                        pool.wait_ge(pool_done, pool_count(g, j, POOL_TILES[n]))
                    pool.tensor_tensor(acc[:, :], (acc if n else probs[0])[:, :], probs[t % RING][:, :], ALU.add) \
                        .then_inc(pool_done, 1)
                pool.wait_ge(added, DVE_OPS * (h + 1))
                pool.wait_ge(pool_done, pool_count(g, j, POOL_TILES[-1]))
                pool.tensor_tensor(acc[:, :], acc[:, :], psum_d[:, :], ALU.add).then_inc(pool_done, 1)

            for j in range(SLOTS):
                period(0, j)
            with pool.Fori(1, HEADS // SLOTS) as g:
                for j in range(SLOTS):
                    period(g, j)

        @block.tensor
        def _(pe):
            pe.wait_ge(ident_done, 2)
            pe.wait_ge(ones_done, 1 + SLOTS)

            def scores_t(g, j, t, b):
                h = number(g, j)
                wait(pe, exp_done, 64 * h + 4 * t + b - ST_BANKS + 1)
                pe.matmul(ps[:, b % ST_BANKS, :], kp[j][0:PACK + 1, t * P:(t + 1) * P],
                          qp[j][0:PACK + 1, b * NQ:(b + 1) * NQ], start=True, stop=True).then_inc(st_ready, 1)

            def scores(g, j, t, b):
                gn, jn = head(g, j, 2)
                n, bank = unit(g, j, t, b)
                wait(pe, mx_free, n - MAX_BANKS + 1)
                pe.matmul(ps[:, MAX_BANK + bank, :], qp[jn][0:PACK, t * P:(t + 1) * P],
                          kp[jn][0:PACK, b * NQ:(b + 1) * NQ], start=True, stop=True).then_inc(mx_ready, 1)

            def transpose_max(g, j):
                gn, jn = head(g, j, 1)
                n, bank = transposed_unit(g, j)
                pe.wait_ge(rowmax_ready, number(gn, jn) + 1)
                pe.wait_ge(mx_free, n - MAX_BANKS + 1)
                pe.transpose(ps[0:TT, MAX_BANK + bank, 0:P], row_max[jn % 2][:, :], ident[:, :]).then_inc(mx_ready, 1)

            def values(g, j, t):
                h = number(g, j)
                pe.wait_ge(exp_done, 64 * h + 4 * t + 4)
                if t == 0:
                    pe.wait_ge(v_loaded[j], 16 * (g + 1))
                    wait(pe, raw_done, h)
                for b in range(QB):
                    last = pe.matmul(ps[b * HD:(b + 1) * HD, PV_BANK, :], vh[j][:, t, :],
                                     probs[t % RING][:, b * NQ:(b + 1) * NQ], start=(t == 0), stop=(t == TT - 1))
                if t not in PE_TILES:
                    last.then_inc(pv_done, 1)

            def sums(g, j, t):
                if t not in PE_TILES:
                    return
                if t == PE_TILES[0]:
                    wait(pe, sums_taken, number(g, j))
                for b in range(QB):
                    last = pe.matmul(ps[b * HD:(b + 1) * HD, SUM_BANK, :], ones[:, :],
                                     probs[t % RING][:, b * NQ:(b + 1) * NQ], start=(t == PE_TILES[0]), stop=False)
                last.then_inc(pv_done, 1)

            def pool_sums(g, j):
                h = number(g, j)
                pe.wait_ge(pool_done, POOL_OPS * (h + 1))
                for b in range(QB):
                    last = pe.matmul(ps[b * HD:(b + 1) * HD, SUM_BANK, :], ones[:, :],
                                     psum_p[j % 2][:, b * NQ:(b + 1) * NQ], start=False, stop=True)
                last.then_inc(sum_ready, 1)

            def period(g, j, attends, has_before, maxima, transposes):
                gb, jb = head(g, j, -1)
                gn, jn = head(g, j, 2)
                if attends:
                    pe.wait_ge(negmax_loaded[j], 16 * (g + 1))
                if maxima:
                    pe.wait_ge(kq_loaded[jn], 16 * 6 * (gn + 1))
                for t in range(TT):
                    late = (gb, jb, TT - 1) if t == 0 else (g, j, t - 1)
                    has_late = has_before if t == 0 else attends
                    for half in range(2):
                        for own, b in ((False, 0), (True, 0), (False, 1), (True, 1)) if half == 0 else \
                                ((True, 2), (False, 2), (True, 3), (False, 3)):
                            if own and attends:
                                scores_t(g, j, t, b)
                            if not own and maxima:
                                scores(g, j, t, b)
                        if half == 0 and has_late:
                            values(*late)
                        if half == 1 and has_late:
                            sums(*late)
                        if half == 1 and t == 2 and has_before:
                            pool_sums(gb, jb)
                    if t == 1 and transposes:
                        transpose_max(g, j)

            scheduled(period)
            with pe.Fori(1, 7) as g:
                for j in range(SLOTS):
                    period(g, j, True, True, True, True)
            for j in range(SLOTS):
                period(7, j, True, True, j < 2, j < 3)
            values(7, 3, TT - 1)
            sums(7, 3, TT - 1)
            pool_sums(7, 3)

        @block.scalar
        def _(act):
            def take_raw(g, j):
                h = number(g, j)
                act.wait_ge(pv_done, 16 * (h + 1))
                wait(act, ctx_ready, h - 1)
                act.activation(raw_ctx[j % 2][:, :], ps[:, PV_BANK, :], ACT.Copy).then_inc(raw_done, 1)

            def take_sums(g, j):
                h = number(g, j)
                act.wait_ge(sum_ready, h + 1)
                wait(act, sums_spread, 16 * QB * h)
                act.activation(sums_b[:, :], ps[:, SUM_BANK, :], ACT.Copy).then_inc(sums_taken, 1)

            def period(g, j, has_before=True):
                h = number(g, j)
                for t in range(TT):
                    gr, jr = (g, j) if t >= RING else head(g, j, -1)
                    tr = (t - RING) % TT
                    if has_before or t >= RING:
                        act.wait_ge(pv_done, 16 * h + t - RING + 1)
                        if tr in POOL_TILES:
                            act.wait_ge(pool_done, pool_count(gr, jr, tr))
                        if tr in DVE_TILES:
                            act.wait_ge(added, added_count(gr, jr, tr))
                    for b in range(QB):
                        act.wait_ge(st_ready, 64 * h + 4 * t + b + 1)
                        act.activation(probs[t % RING][:, b * NQ:(b + 1) * NQ], ps[:, b % ST_BANKS, :],
                                       ACT.Exp, scale=SCALE).then_inc(exp_done, 1)
                        if t == 0 and b == 3 and has_before:
                            take_raw(*head(g, j, -1))
                        if t == 3 and b == 3 and has_before:
                            take_sums(*head(g, j, -1))

            for j in range(SLOTS):
                period(0, j, j > 0)
            with act.Fori(1, HEADS // SLOTS) as g:
                for j in range(SLOTS):
                    period(g, j)
            take_raw(7, 3)
            take_sums(7, 3)

        @block.vector
        def _(dve):
            def take_max(g, j, t, b):
                gn, jn = head(g, j, 2)
                n, bank = unit(g, j, t, b)
                dve.wait_ge(mx_ready, n + 1)
                dve.tensor_reduce(part_max[jn % 2][:, t, b:b + 1], ps[:, MAX_BANK + bank, :], AX_X, ALU.max) \
                    .then_inc(mx_free, 1)

            def take_transposed(g, j):
                gn, jn = head(g, j, 1)
                n, bank = transposed_unit(g, j)
                wait(dve, negmax_loaded[jn], 16 * gn)
                dve.wait_ge(mx_ready, n + 1)
                dve.tensor_scalar(neg_max[jn][:, :].bitcast(F32R), ps[0:TT, MAX_BANK + bank, 0:P], -1.0, None,
                                  ALU.mult).then_inc(mx_free, 1)

            def reciprocal(g, j):
                h = number(g, j)
                dve.wait_ge(sums_spread, 16 * QB * (h + 1))
                wait(dve, recip_stored, 16 * h)
                dve.reciprocal(recip_q[:, :], sums_q[:, :]).then_inc(recip_done, 1)

            def add_tile(g, j, n, part):
                h = number(g, j)
                c = slice(part * NQ, (part + 1) * NQ)
                a, b = DVE_TILES[n], DVE_TILES[n + 1]
                dve.wait_ge(exp_done, 64 * h + 4 * b + 4)
                if n:
                    dve.wait_ge(added, DVE_OPS * h + QB * (n - 1) + part + 1)
                else:
                    wait(dve, pool_done, POOL_OPS * h)
                dve.tensor_tensor(psum_d[:, c], (psum_d if n else probs[a % RING])[:, c],
                                  probs[b % RING][:, c], ALU.add).then_inc(added, 1)

            def normalise(g, j):
                h = number(g, j)
                dve.wait_ge(raw_done, h + 1)
                dve.wait_ge(recip_loaded, 16 * QB * (h + 1))
                wait(dve, ctx_stored[j % 2], 16 * QB * (2 * g + j // 2))
                dve.tensor_tensor(out_ctx[j % 2][:, :], raw_ctx[j % 2][:, :], recip_b[:, :], ALU.mult) \
                    .then_inc(ctx_ready, 1)

            def period(g, j, attends, has_before, maxima, transposes):
                gn, jn = head(g, j, 2)
                for t in range(TT):
                    if maxima:
                        for b in range(QB):
                            take_max(g, j, t, b)
                            if t in ADD_AT and b == 0 and attends:
                                add_tile(g, j, *divmod(ADD_AT.index(t), QB))
                    if not maxima and t in ADD_AT:
                        add_tile(g, j, *divmod(ADD_AT.index(t), QB))
                    if t == 1 and transposes:
                        take_transposed(g, j)
                    if t == RECIPROCAL_AT and has_before:
                        reciprocal(*head(g, j, -1))
                    if t == NORMALISE_AT and has_before:
                        normalise(*head(g, j, -1))
                if maxima:
                    n, _ = unit(g, j, TT - 1, QB - 1)
                    dve.wait_ge(mx_free, n + 1)
                    dve.tensor_reduce(row_max[jn % 2][:, :], part_max[jn % 2][:, :, :], AX_X, ALU.max) \
                        .then_inc(rowmax_ready, 1)

            scheduled(period)
            with dve.Fori(1, 7) as g:
                for j in range(SLOTS):
                    period(g, j, True, True, True, True)
            for j in range(SLOTS):
                period(7, j, True, True, j < 2, j < 3)
            reciprocal(7, 3)
            normalise(7, 3)


def project_output(nc, x, w2, bias, cz_scr, out):
    with ExitStack() as ctx:
        def sb(name, shape, dt=F32):
            return ctx.enter_context(nc.sbuf_tensor(name, shape, dt))

        def sem(name):
            return ctx.enter_context(nc.semaphore(name))

        whi = sb("w2hi", [P, OUT_KT, D], F32R)
        wlo = sb("w2lo", [P, OUT_KT, D], F32R)
        wraw = sb("w2raw", [P, 2, D])
        craw = sb("craw", [P, 2, OUT_KT, P])
        chi = sb("chi", [P, 2, OUT_KT, P], F32R)
        clo = sb("clo", [P, 2, OUT_KT, P], F32R)
        xt = sb("xt", [P, 2, D])
        ob = sb("ob", [P, D])
        res = sb("res", [P, 2, D])
        ps = ctx.enter_context(nc.psum_tensor("ps_c", [P, 8, NQ], F32))

        w_loaded = [sem("w2_loaded0"), sem("w2_loaded1")]
        whi_done = sem("w2hi_done")
        wlo_done = sem("w2lo_done")
        c_loaded = [sem("c_loaded0"), sem("c_loaded1")]
        x_loaded = [sem("xc_loaded0"), sem("xc_loaded1")]
        ob_loaded = sem("ob_loaded")
        chi_done = sem("chi_done")
        clo_done = sem("clo_done")
        xb_done = sem("xb_done")
        mm_ready = sem("c_mm_ready")
        res_ready = sem("res_ready")
        out_stored = [sem("out_stored0"), sem("out_stored1")]
        block = ctx.enter_context(nc.Block())

        @block.sync
        def _(sp):
            def load(i, u):
                tok = bass.ds((2 * i + u) * P, P)
                sp.dma_start(craw[:, u, :, :], cz_scr[:, tok].rearrange("(k p) t -> p k t", p=P)) \
                    .then_inc(c_loaded[u], 16)
                sp.dma_start(xt[:, u, :], x[tok, :]).then_inc(x_loaded[u], 16)

            for k in range(2):
                sp.dma_start(wraw[:, k, :], w2[k * P:(k + 1) * P, :]).then_inc(w_loaded[k], 16)
            sp.dma_start(ob[:, :], bias.partition_broadcast(P)).then_inc(ob_loaded, 16)
            for u in range(2):
                load(0, u)
            for k in range(2, OUT_KT):
                sp.wait_ge(wlo_done, k - 1)
                sp.dma_start(wraw[:, k % 2, :], w2[k * P:(k + 1) * P, :]).then_inc(w_loaded[k % 2], 16)
            with sp.Fori(0, TT // 2 - 1) as i:
                for u in range(2):
                    n = 2 * i + u + 1
                    sp.wait_ge(clo_done, n)
                    sp.wait_ge(res_ready, n)
                    load(i + 1, u)
                    sp.dma_start(out[bass.ds((2 * i + u) * P, P), :], res[:, u, :]).then_inc(out_stored[u], 16)
            for u in range(2):
                n = TT - 1 + u
                sp.wait_ge(res_ready, n)
                sp.dma_start(out[(n - 1) * P:n * P, :], res[:, u, :]).then_inc(out_stored[u], 16)
            for u in range(2):
                sp.wait_ge(out_stored[u], 16 * TT // 2)

        @block.gpsimd
        def _(pool):
            pool.wait_ge(ob_loaded, 16)
            with pool.Fori(0, TT // 2) as i:
                for u in range(2):
                    pool.wait_ge(x_loaded[u], 16 * (i + 1))
                    pool.tensor_tensor(xt[:, u, :], xt[:, u, :], ob[:, :], ALU.add).then_inc(xb_done, 1)

        @block.tensor
        def _(pe):
            def tile(i, u, first=False):
                pe.wait_ge(chi_done, 2 * i + u + 1)
                pe.wait_ge(clo_done, 2 * i + u + 1)
                wait(pe, res_ready, 2 * i + u - 1)
                n = 0
                for k in range(OUT_KT):
                    if first:
                        pe.wait_ge(whi_done, k + 1)
                        pe.wait_ge(wlo_done, k + 1)
                    for c, w in ((chi, whi), (chi, wlo), (clo, whi)):
                        for b in range(2):
                            last = pe.matmul(ps[:, 2 * u + b, :], c[:, u, k, :], w[:, k, b * NQ:(b + 1) * NQ],
                                             start=(n == 0), stop=(n == 3 * OUT_KT - 1))
                        n += 1
                last.then_inc(mm_ready, 1)

            tile(0, 0, True)
            tile(0, 1)
            with pe.Fori(1, TT // 2) as i:
                for u in range(2):
                    tile(i, u)

        @block.scalar
        def _(act):
            def split(i, u):
                act.wait_ge(c_loaded[u], 16 * (i + 1))
                wait(act, mm_ready, 2 * i + u - 1)
                act.activation(chi[:, u, :, :], craw[:, u, :, :], ACT.Copy).then_inc(chi_done, 1)

            def split_w(k):
                act.wait_ge(w_loaded[k % 2], 16 * (k // 2 + 1))
                act.activation(whi[:, k, :], wraw[:, k % 2, :], ACT.Copy).then_inc(whi_done, 1)

            split_w(0)
            split_w(1)
            for u in range(2):
                split(0, u)
            for k in range(2, OUT_KT):
                split_w(k)
            with act.Fori(1, TT // 2) as i:
                for u in range(2):
                    split(i, u)

        @block.vector
        def _(dve):
            def split(i, u):
                dve.wait_ge(chi_done, 2 * i + u + 1)
                dve.tensor_tensor(clo[:, u, :, :], craw[:, u, :, :], chi[:, u, :, :].bitcast(F32), ALU.subtract) \
                    .then_inc(clo_done, 1)

            def split_w(k):
                dve.wait_ge(whi_done, k + 1)
                dve.tensor_tensor(wlo[:, k, :], wraw[:, k % 2, :], whi[:, k, :].bitcast(F32), ALU.subtract) \
                    .then_inc(wlo_done, 1)

            def finish(i, u):
                dve.wait_ge(mm_ready, 2 * i + u + 1)
                dve.wait_ge(xb_done, 2 * i + u + 1)
                wait(dve, out_stored[u], 16 * i)
                dve.tensor_tensor(res[:, u, :], ps[:, 2 * u:2 * u + 2, :].rearrange("p b n -> p (b n)"),
                                  xt[:, u, :], ALU.add).then_inc(res_ready, 1)

            split_w(0)
            split_w(1)
            for u in range(2):
                split(0, u)
            for k in range(2, OUT_KT):
                split_w(k)
            for u in range(2):
                finish(0, u)
                split(1, u)
            with dve.Fori(1, TT // 2 - 1) as i:
                for u in range(2):
                    finish(i, u)
                    split(i + 1, u)
            for u in range(2):
                finish(TT // 2 - 1, u)


def build(nc, x, wcat, keys_t, w2, bias, out):
    qk_scr = nc.dram_tensor("qk_scr", [2, 2 * D, T], F32, kind="Internal").ap()
    v_scr = nc.dram_tensor("v_scr", [V_BLOCKS, P, T], F32, kind="Internal").ap()
    gate_scr = nc.dram_tensor("gate_scr", [EXPERTS, T], F32, kind="Internal").ap()
    recip_scr = nc.dram_tensor("recip_scr", [T], F32, kind="Internal").ap()
    cz_scr = nc.dram_tensor("cz_scr", [D + BOTTLENECK, T], F32, kind="Internal").ap()
    project_inputs(nc, x, wcat, keys_t, qk_scr, v_scr, gate_scr, cz_scr)
    attend(nc, qk_scr, v_scr, recip_scr, cz_scr)
    project_output(nc, x, w2, bias, cz_scr, out)


def kernel(**inputs):
    import numpy as np
    import concourse.bacc as bacc
    from concourse.bass_utils import run_bass_kernel_spmd

    x = np.ascontiguousarray(inputs["L0_attn_x"]).reshape(T, D)
    qkvw = np.asarray(inputs["L0_attn_attn_qkvw"])
    qkvb = np.asarray(inputs["L0_attn_attn_qkvb"])
    router = np.zeros((D, P), np.float32)
    router[:, :ROUTER] = np.asarray(inputs["L0_ffn_Wq_w"]).T
    cols = np.concatenate([router, qkvw, np.asarray(inputs["L0_ffn_A_w"]).T], axis=1)
    wcat = np.zeros((BLOCKS, P, WROW), np.float32)
    wcat[:, :, :KT * P] = cols.reshape(KT, P, BLOCKS, P).transpose(2, 1, 0, 3).reshape(BLOCKS, P, KT * P)
    wcat[1:Z0, :, KT * P] = qkvb.reshape(Z0 - 1, P)
    arrays = {
        "x": x,
        "wcat": wcat,
        "keys_t": np.ascontiguousarray(np.asarray(inputs["L0_ffn_keys"]).T),
        "w2": np.concatenate([np.asarray(inputs["L0_attn_attn_ow"]), np.asarray(inputs["L0_ffn_B_w"]).T], axis=0),
        "bias": np.ascontiguousarray(inputs["L0_attn_attn_ob"]),
    }
    nc = bacc.Bacc("TRN2", target_bir_lowering=False, num_devices=1)
    aps = [nc.dram_tensor(n, a.shape, F32, kind="ExternalInput").ap() for n, a in arrays.items()]
    out = nc.dram_tensor("out", [T, D], F32, kind="ExternalOutput").ap()
    build(nc, *aps, out)
    r = run_bass_kernel_spmd(nc, [arrays], core_ids=[0])
    return r.results[0]["out"].reshape(1, T, D)
```

```python
from contextlib import ExitStack

import concourse.bass as bass
from concourse import mybir

F32 = mybir.dt.float32
F32R = mybir.dt.float32r
ALU = mybir.AluOpType
ACT = mybir.ActivationFunctionType
AX_X = mybir.AxisListType.X

P = 128
T = 2048
D = 1024
HEADS = 32
HD = D // HEADS
SCALE = HD ** -0.5
EPS = 1e-5
KT = D // P
TT = T // P
NQ = 512
QB = T // NQ
CHUNK = NQ // P
EXPERTS = 64
RANK = 8
BOTTLENECK = EXPERTS * RANK
ROUTER = 16
SCALING = 2.0
LOWEST = -3.0e38

ROUTER_BLOCK = 0
QK_BLOCKS = 2 * D // P
V_BLOCKS = D // P
Z_BLOCKS = BOTTLENECK // P
V0 = 1 + QK_BLOCKS
Z0 = V0 + V_BLOCKS
BLOCKS = Z0 + Z_BLOCKS
WROW = KT * P + 1

PACK = 3 * HD

POOL_TILES = [0, 1, 2, 4, 6, 9, 11, 12, 13, 14]
DVE_TILES = [3, 5, 8]
LAST_POOL_TILES = [0, 1, 2, 4, 6, 8]
LAST_DVE_TILES = [3, 5, 7, 9, 10, 11]
POOL_OPS = len(POOL_TILES)
DVE_OPS = QB * (len(DVE_TILES) - 1)
ADD_AT = [(6, 1), (7, 1), (8, 1), (8, 3), (9, 1), (10, 1), (11, 1), (12, 1)]
LEAD = 3
POOL_SUMS_AT, TAKE_SUMS_AT, RECIPROCAL_AT, NORMALISE_AT = 3, 4, 8, 10
RING = 8
SLOTS = 4

OUT_KT = KT + Z_BLOCKS
EARLY = 6


def wait(eng, sem, value):
    if isinstance(value, int) and value <= 0:
        return
    eng.wait_ge(sem, value)


def project_inputs(nc, x, wcat, keys_t, qk_scr, v_scr, gate_scr, cz_scr):
    with ExitStack() as ctx:
        def sb(name, shape, dt=F32):
            return ctx.enter_context(nc.sbuf_tensor(name, shape, dt))

        def sem(name):
            return ctx.enter_context(nc.semaphore(name))

        xhi = sb("xhi", [P, KT, T], F32R)
        xlo = sb("xlo", [P, KT, T], F32R)
        wraw = sb("wraw", [P, 2, WROW])
        whi = sb("whi", [P, 2, KT * P], F32R)
        wlo = sb("wlo", [P, 2, KT * P], F32R)
        ehi = sb("ehi", [P, 2, T])
        elo = sb("elo", [P, 2, T])
        stage = sb("stage", [P, 2 * T])
        ident = sb("ident", [P, P])
        keys = sb("keys", [ROUTER, EXPERTS])
        stats = sb("stats", [P, CHUNK, 2, 6])
        mv = sb("mv", [P, CHUNK, 2])
        std = sb("std", [P, CHUNK, 2])
        top = sb("top", [P, TT, 16])
        gsum = sb("gsum", [P, TT, 2])
        ps = ctx.enter_context(nc.psum_tensor("ps_a", [P, 8, NQ], F32))
        ps_flat = ps[:, :, :].rearrange("p b n -> p (b n)")

        x_in = stage[:, :].rearrange("p (s d) -> p s d", s=CHUNK)
        xn = ehi[:, :, :].rearrange("p u (v d) -> p (u v) d", v=2)
        qr_t = elo[0:ROUTER, 1, :]
        sc_flat = stage[:, T:T + TT * EXPERTS]
        sc = sc_flat.rearrange("p (t e) -> p t e", e=EXPERTS)
        left_flat = stage[:, T + TT * EXPERTS:T + 2 * TT * EXPERTS]
        left = left_flat.rearrange("p (t e) -> p t e", e=EXPERTS)
        gate_t = stage[0:EXPERTS, 0:T]
        gates = stage[:, :].rearrange("p (u t) -> p u t", u=2)

        x_loaded = [sem(f"x_loaded{i}") for i in range(CHUNK)]
        ident_done = sem("ident_done")
        keys_loaded = sem("keys_loaded")
        stats_done = sem("stats_done")
        stats_seen = sem("stats_seen")
        mean_done = sem("mean_done")
        var_ready = sem("var_ready")
        std_ready = sem("std_ready")
        rstd_done = sem("rstd_done")
        xn_ready = sem("xn_ready")
        xt_ready = sem("xt_ready")
        xhi_done = sem("xhi_done")
        xlo_done = sem("xlo_done")
        w_loaded = [sem("w_loaded0"), sem("w_loaded1")]
        whi_done = sem("whi_done")
        wlo_done = sem("wlo_done")
        mm_ready = sem("mm_ready")
        hi_done = sem("hi_done")
        lo_done = sem("lo_done")
        stored = [sem("stored0"), sem("stored1")]
        score_ready = sem("score_ready")
        top_step = sem("top_step")
        shifted_ready = sem("shifted_ready")
        gexp_ready = sem("gexp_ready")
        gate_ready = sem("gate_ready")
        gtr_ready = sem("gtr_ready")
        gate_t_ready = sem("gate_t_ready")
        gate_stored = sem("gate_stored")
        gates_loaded = [sem("gates_loaded0"), sem("gates_loaded1")]
        vtr_ready = sem("vtr_ready")

        def quarter(blk, nb):
            return 4 * blk + nb + 1

        def product(blk, nb):
            return 2 * nb + blk + 1 if isinstance(blk, int) and blk < 2 else quarter(blk, nb)

        def hi_count(blk, nb):
            return 4 * blk + nb - 3

        def transposed(t):
            u = t % 2
            return ps[:, 4 + 2 * u:6 + 2 * u, :].rearrange("p b (k n) -> p (b k) n", n=P)

        def pair(i):
            return [(u, 2 * i + u + 1) for u in range(2)]

        block = ctx.enter_context(nc.Block())

        @block.sync
        def _(sp):
            def load_w(blk, slot):
                sp.dma_start(wraw[:, slot, :], wcat[bass.ds(blk, 1), :, :].rearrange("a p n -> (a p) n")) \
                    .then_inc(w_loaded[slot], 16)

            def load_gates(b, u):
                for r in range(RANK):
                    sp.dma_start(gates[r::RANK, u, :], gate_scr[16 * b:16 * b + 16, :]) \
                        .then_inc(gates_loaded[u], 16)

            def store_qk(blk, u):
                row = (blk - 1) * P
                for part, ev in ((0, ehi), (1, elo)):
                    sp.dma_start(qk_scr[part, bass.ds(row, P), :], ev[:, u, :]).then_inc(stored[u], 16)

            for t in range(CHUNK):
                sp.dma_start(x_in[:, t, :], x[t * P:(t + 1) * P, :]).then_inc(x_loaded[t], 16)
            load_w(0, 0)
            load_w(1, 1)
            sp.dma_start(keys[:, :], keys_t).then_inc(keys_loaded, 16)
            with sp.Fori(1, QB) as c:
                for t in range(CHUNK):
                    sp.wait_ge(xn_ready, CHUNK * c + t - CHUNK + 1)
                    sp.dma_start(x_in[:, t, :], x[bass.ds((CHUNK * c + t) * P, P), :]).then_inc(x_loaded[t], 16)
            sp.wait_ge(wlo_done, 1)
            load_w(2, 0)

            def after_qk(i):
                for u, blk in pair(i):
                    sp.wait_ge(lo_done, quarter(blk, 3))
                    store_qk(blk, u)
                    load_w(blk + 2, (u + 1) % 2)

            after_qk(0)
            sp.wait_ge(gate_t_ready, 1)
            sp.dma_start(gate_scr, gate_t).then_inc(gate_stored, 16)
            with sp.Fori(1, QK_BLOCKS // 2) as i:
                after_qk(i)
            sp.wait_ge(gate_stored, 16)
            for u in range(2):
                load_gates(u, u)
            with sp.Fori(QK_BLOCKS // 2, (QK_BLOCKS + V_BLOCKS) // 2) as i:
                for u, blk in pair(i):
                    sp.wait_ge(lo_done, quarter(blk, 3))
                    vb = blk - V0
                    for half in range(2):
                        c = slice(half * T // 2, (half + 1) * T // 2)
                        sp.dma_start(v_scr[bass.ds(vb, 1), :, c].rearrange("a p n -> (a p) n"), elo[:, u, c]) \
                            .then_inc(stored[u], 16)
                    load_w(blk + 2, (u + 1) % 2)
            for b in range(Z_BLOCKS):
                blk, u = Z0 + b, b % 2
                sp.wait_ge(lo_done, quarter(blk, 3))
                for half in range(2):
                    c = slice(half * T // 2, (half + 1) * T // 2)
                    sp.dma_start(cz_scr[D + b * P:D + (b + 1) * P, c], elo[:, u, c]).then_inc(stored[u], 16)
                if blk + 2 < BLOCKS:
                    load_w(blk + 2, (u + 1) % 2)
                    load_gates(b + 2, u)
            for u in range(2):
                sp.wait_ge(stored[u], 32 * (BLOCKS - 1) // 2)

        @block.gpsimd
        def _(pool):
            pool.memset(ident[:, :], 0.0).then_inc(ident_done, 1)
            pool.wait_ge(ident_done, 1)
            pool.affine_select(out=ident[:, :], in_=ident[:, :], compare_op=ALU.not_equal, fill=1.0,
                               base=0, pattern=[[-1, P]], channel_multiplier=1).then_inc(ident_done, 1)

            def split(blk, slot):
                pool.wait_ge(whi_done, blk + 1)
                pool.tensor_tensor(wlo[:, slot, :], wraw[:, slot, 0:KT * P], whi[:, slot, :].bitcast(F32),
                                   ALU.subtract).then_inc(wlo_done, 1)

            split(0, 0)
            with pool.Fori(0, (BLOCKS - 1) // 2) as i:
                for u, blk in pair(i):
                    split(blk, (u + 1) % 2)

        @block.tensor
        def _(pe):
            pe.wait_ge(ident_done, 2)

            def transpose_x(c, half):
                for t in (2 * half, 2 * half + 1):
                    n = CHUNK * c + t
                    pe.wait_ge(xn_ready, n + 1)
                    wait(pe, xlo_done, n - 1)
                    for k in range(KT):
                        last = pe.transpose(ps[:, 4 + 2 * (t % 2) + k // 4, (k % 4) * P:(k % 4 + 1) * P],
                                            xn[:, t, k * P:(k + 1) * P], ident[:, :])
                    last.then_inc(xt_ready, 1)

            def project(slot, nb):
                n = 0
                tk = bass.ds(nb * NQ, NQ)
                for k in range(KT):
                    wk = slice(k * P, (k + 1) * P)
                    for w, xx in ((whi, xhi), (whi, xlo), (wlo, xhi)):
                        last = pe.matmul(ps_flat[:, tk], w[:, slot, wk], xx[:, k, tk],
                                         start=(n == 0), stop=(n == 3 * KT - 1))
                        n += 1
                last.then_inc(mm_ready, 1)

            def qk_block(u, blk):
                pe.wait_ge(wlo_done, blk + 1)
                for nb in range(QB):
                    wait(pe, lo_done, quarter(blk - 1, nb))
                    project((u + 1) % 2, nb)

            def first_block(blk, c):
                pe.wait_ge(wlo_done, blk + 1)
                if blk == 0:
                    pe.wait_ge(xhi_done, CHUNK * (c + 1))
                    pe.wait_ge(xlo_done, CHUNK * (c + 1))
                else:
                    pe.wait_ge(lo_done, c + 1)
                project(blk, c)

            for half in range(2):
                transpose_x(0, half)
            with pe.Fori(1, QB) as c:
                for blk in range(2):
                    transpose_x(c, blk)
                    first_block(blk, c - 1)
            for blk in range(2):
                first_block(blk, QB - 1)

            pe.wait_ge(lo_done, quarter(0, 3))
            pe.wait_ge(keys_loaded, 16)
            for t in range(TT):
                last = pe.matmul(ps[:, 6 + t // 8, (t % 8) * EXPERTS:(t % 8 + 1) * EXPERTS],
                                 qr_t[:, t * P:(t + 1) * P], keys[:, :], start=True, stop=True)
            last.then_inc(score_ready, 1)
            qk_block(1, 2)
            pe.wait_ge(gate_ready, 1)
            for t in range(TT):
                last = pe.transpose(ps[0:EXPERTS, 4 + t // 4, (t % 4) * P:(t % 4 + 1) * P], sc[:, t, :], ident[:, :])
            last.then_inc(gtr_ready, 1)
            with pe.Fori(1, QK_BLOCKS // 2) as i:
                for u, blk in pair(i):
                    qk_block(u, blk)
            pe.wait_ge(gate_t_ready, 1)

            def transpose_v(u, blk, nb):
                pe.wait_ge(hi_done, hi_count(blk, nb))
                pe.wait_ge(lo_done, quarter(blk, nb) - 2)
                for t in range(4):
                    c = slice(nb * NQ + t * P, nb * NQ + (t + 1) * P)
                    last = pe.transpose(ps[:, 4 + nb % 2, t * P:(t + 1) * P], ehi[:, u, c], ident[:, :])
                last.then_inc(vtr_ready, 1)

            with pe.Fori(QK_BLOCKS // 2, (QK_BLOCKS + V_BLOCKS) // 2) as i:
                for u, blk in pair(i):
                    pe.wait_ge(wlo_done, blk + 1)
                    for nb in range(QB):
                        pe.wait_ge(lo_done, quarter(V0 - 1, nb))
                        pe.wait_ge(hi_done, hi_count(blk - 1, nb))
                        project((u + 1) % 2, nb)
                        if nb >= 1:
                            transpose_v(u, blk, nb - 1)
                    transpose_v(u, blk, QB - 1)
            for b in range(Z_BLOCKS):
                qk_block(b % 2, Z0 + b)

        @block.scalar
        def _(act):
            def round_w(blk, slot, loads):
                act.wait_ge(w_loaded[slot], 16 * loads)
                if not isinstance(blk, int) or blk >= 2:
                    act.wait_ge(mm_ready, product(blk - 2, 3))
                act.activation(whi[:, slot, :], wraw[:, slot, 0:KT * P], ACT.Copy).then_inc(whi_done, 1)

            def deviation(c, half):
                for t in (2 * half, 2 * half + 1):
                    act.wait_ge(var_ready, CHUNK * c + t + 1)
                    act.activation(std[:, t, 0:1], mv[:, t, 1:2], ACT.Sqrt).then_inc(std_ready, 1)

            def round_x(c, half):
                for t in (2 * half, 2 * half + 1):
                    act.wait_ge(xt_ready, CHUNK * c + t + 1)
                    act.activation(xhi[:, :, bass.ds((CHUNK * c + t) * P, P)], transposed(t), ACT.Copy) \
                        .then_inc(xhi_done, 1)

            deviation(0, 0)
            deviation(0, 1)
            round_x(0, 0)
            round_w(0, 0, 1)
            round_w(1, 1, 1)
            with act.Fori(1, QB) as c:
                deviation(c, 0)
                round_x(c - 1, 1)
                deviation(c, 1)
                round_x(c, 0)
            round_x(QB - 1, 1)

            def high_part(u, blk, nb, rounded):
                c = slice(nb * NQ, (nb + 1) * NQ)
                act.wait_ge(mm_ready, product(blk, nb))
                dst = ehi[:, u, c].bitcast(F32R) if rounded else ehi[:, u, c]
                act.activation(dst, ps[:, nb, :], ACT.Identity,
                               bias=wraw[:, (u + 1) % 2, KT * P:WROW]).then_inc(hi_done, 1)

            def part(i, rounded):
                for u, blk in pair(i):
                    act.wait_ge(stored[u], 32 * i)
                    for nb in range(QB):
                        if nb == 1:
                            round_w(blk + 1, u, i + 2)
                        high_part(u, blk, nb, rounded)

            for u, blk in pair(0):
                for nb in range(QB):
                    if nb == QB - 1 - 2 * u:
                        round_w(blk + 1, u, 2)
                    high_part(u, blk, nb, True)
                if u == 0:
                    act.wait_ge(shifted_ready, 1)
                    act.activation(sc_flat, sc_flat, ACT.Exp).then_inc(gexp_ready, 1)
            with act.Fori(1, QK_BLOCKS // 2) as i:
                part(i, True)
            with act.Fori(QK_BLOCKS // 2, (QK_BLOCKS + V_BLOCKS) // 2) as i:
                part(i, False)
            for blk in range(Z0 + 1, BLOCKS):
                round_w(blk, blk % 2, blk // 2 + 1)

        @block.vector
        def _(dve):
            def normalise(c, half):
                for t in (2 * half, 2 * half + 1):
                    n = CHUNK * c + t
                    dve.wait_ge(x_loaded[t], 16 * (c + 1))
                    for part in range(2):
                        dve.bn_stats(stats[:, t, part, :], x_in[:, t, part * 512:(part + 1) * 512]) \
                            .then_inc(stats_done, 1)
                    dve.wait_ge(stats_done, 2 * n + 2)
                    dve.sem_inc(stats_seen, 1)
                    dve.bn_aggr(mv[:, t, :], stats[:, t, :, :]).then_inc(mean_done, 1)
                    dve.wait_ge(mean_done, n + 1)
                    dve.tensor_scalar(mv[:, t, 1:2], mv[:, t, 1:2], EPS, None, ALU.add).then_inc(var_ready, 1)
                for t in (2 * half, 2 * half + 1):
                    n = CHUNK * c + t
                    dve.wait_ge(std_ready, n + 1)
                    dve.reciprocal(std[:, t, 1:2], std[:, t, 0:1]).then_inc(rstd_done, 1)
                    dve.wait_ge(rstd_done, n + 1)
                    wait(dve, xt_ready, n - CHUNK + 1)
                    dve.tensor_scalar(xn[:, t, :], x_in[:, t, :], mv[:, t, 0:1], std[:, t, 1:2],
                                      ALU.subtract, ALU.mult).then_inc(xn_ready, 1)

            def rest_x(c, half):
                for t in (2 * half, 2 * half + 1):
                    n = CHUNK * c + t
                    dve.wait_ge(xhi_done, n + 1)
                    tok = bass.ds(n * P, P)
                    dve.tensor_tensor(xlo[:, :, tok], transposed(t), xhi[:, :, tok].bitcast(F32), ALU.subtract) \
                        .then_inc(xlo_done, 1)

            def router_query(c):
                dve.wait_ge(mm_ready, product(0, c))
                tok = bass.ds(c * NQ, NQ)
                dve.tensor_copy(qr_t[:, tok], ps_flat[0:ROUTER, tok]).then_inc(lo_done, 1)

            normalise(0, 0)
            normalise(0, 1)
            rest_x(0, 0)
            with dve.Fori(1, QB) as c:
                normalise(c, 0)
                rest_x(c - 1, 1)
                normalise(c, 1)
                rest_x(c, 0)
                router_query(c - 1)
            rest_x(QB - 1, 1)
            router_query(QB - 1)

            def rest(u, blk):
                for nb in range(QB):
                    c = slice(nb * NQ, (nb + 1) * NQ)
                    dve.wait_ge(hi_done, hi_count(blk, nb))
                    dve.scalar_tensor_tensor(out=elo[:, u, c].bitcast(F32R), in0=ps[:, nb, :],
                                             scalar=wraw[:, (u + 1) % 2, KT * P:WROW], in1=ehi[:, u, c],
                                             op0=ALU.add, op1=ALU.subtract).then_inc(lo_done, 1)

            rest(0, 1)

            steps = [0]

            def done(ins):
                steps[0] += 1
                ins.then_inc(top_step, 1)

            def before():
                dve.wait_ge(top_step, steps[0])

            dve.wait_ge(score_ready, 1)
            done(dve.tensor_copy(sc_flat, ps[:, 6:8, :].rearrange("p b n -> p (b n)")))
            before()
            for t in range(TT):
                done(dve.max(top[:, t, 0:8], sc[:, t, :]))
            before()
            for t in range(TT):
                done(dve.match_replace(left[:, t, :], top[:, t, 0:8], sc[:, t, :], LOWEST))
            before()
            for t in range(TT):
                done(dve.max(top[:, t, 8:16], left[:, t, :]))
            before()
            for t in range(TT):
                done(dve.match_replace(left[:, t, :], top[:, t, 8:16], left[:, t, :], LOWEST))
            before()
            done(dve.tensor_tensor(left_flat, left_flat, sc_flat, ALU.not_equal))
            before()
            dve.tensor_tensor(sc, sc, top[:, :, 0:1].broadcast_to([P, TT, EXPERTS]), ALU.subtract) \
                .then_inc(shifted_ready, 1)
            dve.wait_ge(gexp_ready, 1)
            done(dve.tensor_tensor(sc_flat, sc_flat, left_flat, ALU.mult))
            before()
            done(dve.tensor_reduce(gsum[:, :, 0:1], sc, AX_X, ALU.add))
            before()
            done(dve.reciprocal(gsum[:, :, 1:2], gsum[:, :, 0:1]))
            before()
            done(dve.tensor_scalar(gsum[:, :, 0:1], gsum[:, :, 1:2], SCALING, None, ALU.mult))
            before()
            dve.tensor_tensor(sc, sc, gsum[:, :, 0:1].broadcast_to([P, TT, EXPERTS]), ALU.mult) \
                .then_inc(gate_ready, 1)

            rest(1, 2)
            dve.wait_ge(gtr_ready, 1)
            dve.tensor_copy(gate_t, ps[0:EXPERTS, 4:8, :].rearrange("p b n -> p (b n)")).then_inc(gate_t_ready, 1)
            with dve.Fori(1, QK_BLOCKS // 2) as i:
                for u, blk in pair(i):
                    dve.wait_ge(stored[u], 32 * i)
                    rest(u, blk)
            with dve.Fori(QK_BLOCKS // 2, (QK_BLOCKS + V_BLOCKS) // 2) as i:
                for u, blk in pair(i):
                    dve.wait_ge(stored[u], 32 * i)
                    for nb in range(QB):
                        dve.wait_ge(vtr_ready, quarter(blk - V0, nb))
                        dve.tensor_copy(elo[:, u, nb * NQ:(nb + 1) * NQ], ps[:, 4 + nb % 2, :]).then_inc(lo_done, 1)
            for b in range(Z_BLOCKS):
                blk, u = Z0 + b, b % 2
                dve.wait_ge(stored[u], 32 * ((blk - 1) // 2))
                dve.wait_ge(gates_loaded[u], 16 * RANK * (b // 2 + 1))
                for nb in range(QB):
                    c = slice(nb * NQ, (nb + 1) * NQ)
                    dve.wait_ge(mm_ready, quarter(blk, nb))
                    dve.tensor_tensor(elo[:, u, c], ps[:, nb, :], gates[:, u, c], ALU.mult).then_inc(lo_done, 1)


def attend(nc, qk_scr, v_scr, recip_scr, cz_scr, w2, w_early, early_loaded):
    with ExitStack() as ctx:
        def sb(name, shape, dt=F32):
            return ctx.enter_context(nc.sbuf_tensor(name, shape, dt))

        def sem(name):
            return ctx.enter_context(nc.semaphore(name))

        kp = [sb(f"kp{s}", [P, T], F32R) for s in range(SLOTS)]
        qp = [sb(f"qp{s}", [P, T], F32R) for s in range(SLOTS)]
        vh = [sb(f"vh{s}", [P, TT, HD]) for s in range(SLOTS)]
        probs = [sb(f"probs{s}", [P, T]) for s in range(RING)]
        psum_d = sb("psum_d", [P, T])
        psum_p = [sb(f"psum_p{s}", [P, T]) for s in range(2)]
        raw_ctx = [sb(f"raw_ctx{s}", [P, NQ]) for s in range(2)]
        out_ctx = [sb(f"out_ctx{s}", [P, NQ]) for s in range(2)]
        sums_b = sb("sums_b", [P, NQ])
        sums_q = sb("sums_q", [P, T // P])
        recip_q = sb("recip_q", [P, T // P])
        recip_b = sb("recip_b", [P, NQ])
        part_max = [sb(f"part_max{s}", [P, TT, QB]) for s in range(2)]
        row_max = [sb(f"row_max{s}", [P, TT]) for s in range(2)]
        neg_max = [sb(f"neg_max{s}", [TT, P]) for s in range(SLOTS)]
        ones = sb("ones", [P, HD])
        ident = sb("ident_b", [P, P])
        ps = ctx.enter_context(nc.psum_tensor("ps_b", [P, 8, NQ], F32))
        ST_BANKS, MAX_BANKS = 2, 4
        MAX_BANK, PV_BANK, SUM_BANK = 2, 6, 7

        ident_done = sem("b_ident_done")
        ones_done = sem("ones_done")
        kq_loaded = [sem(f"kq_loaded{s}") for s in range(SLOTS)]
        v_loaded = [sem(f"v_loaded{s}") for s in range(SLOTS)]
        negmax_loaded = [sem(f"negmax_loaded{s}") for s in range(SLOTS)]
        st_ready = sem("st_ready")
        exp_done = sem("exp_done")
        pv_done = sem("pv_done")
        pool_done = sem("pool_done")
        added = sem("added")
        mx_ready = sem("mx_ready")
        mx_free = sem("mx_free")
        rowmax_ready = sem("rowmax_ready")
        raw_done = sem("raw_done")
        sum_ready = sem("sum_ready")
        sums_taken = sem("sums_taken")
        sums_spread = sem("sums_spread")
        recip_done = sem("recip_done")
        recip_stored = sem("recip_stored")
        recip_loaded = sem("recip_loaded")
        ctx_ready = sem("ctx_ready")
        ctx_stored = [sem("ctx_stored0"), sem("ctx_stored1")]

        TRANSPOSED_AT = TT - LEAD
        UNITS = QB * TT + 1
        LAST = (HEADS // SLOTS - 1, SLOTS - 1)

        def head(g, j, ahead=0):
            return g + (j + ahead) // SLOTS, (j + ahead) % SLOTS

        def number(g, j):
            return SLOTS * g + j

        def is_last(g, j):
            return isinstance(g, int) and (g, j) == LAST

        def st_bank(g, j, b):
            return b % (QB if is_last(g, j) else ST_BANKS)

        def target(g, j, t):
            return (*head(g, j, 1 if t + LEAD < TT else 2), (t + LEAD) % TT)

        def has_maxima(g, j, t):
            return not isinstance(g, int) or number(*target(g, j, t)[:2]) < HEADS

        def unit(g, j, t, b):
            r = QB * (TT + LEAD) + 1 + QB * t + b + (1 if t > TRANSPOSED_AT else 0)
            return SLOTS * UNITS * g + UNITS * j + r, (UNITS * j + r) % MAX_BANKS

        def transposed_unit(g, j):
            return unit(g, j, TRANSPOSED_AT, QB if has_maxima(g, j, TRANSPOSED_AT) else 0)

        def tiles(g, j):
            by_pool, by_dve = (LAST_POOL_TILES, LAST_DVE_TILES) if is_last(g, j) else (POOL_TILES, DVE_TILES)
            return by_pool, by_dve, [t for t in range(TT) if t not in by_pool + by_dve]

        def pool_count(g, j, t):
            return POOL_OPS * number(g, j) + max(1, tiles(g, j)[0].index(t))

        def added_count(g, j, t):
            return DVE_OPS * number(g, j) + QB * max(1, tiles(g, j)[1].index(t))

        def scheduled(engine, body):
            body(-1, SLOTS - 1, False, False)
            for j in range(SLOTS):
                body(0, j, True, j > 0)
            with engine.Fori(1, LAST[0]) as g:
                for j in range(SLOTS):
                    body(g, j, True, True)
            for j in range(SLOTS):
                body(LAST[0], j, True, True)

        block = ctx.enter_context(nc.Block())

        @block.sync
        def _(sp):
            def load(g, j):
                h = number(g, j)
                q_row, k_row = h * HD, h * HD + D
                for r, hl in enumerate((0, 1, 0)):
                    sp.dma_start(kp[j][r * HD:(r + 1) * HD, :].bitcast(F32), qk_scr[hl, bass.ds(k_row, HD), :]) \
                        .then_inc(kq_loaded[j], 16)
                for r, hl in enumerate((0, 0, 1)):
                    sp.dma_start(qp[j][r * HD:(r + 1) * HD, :].bitcast(F32), qk_scr[hl, bass.ds(q_row, HD), :]) \
                        .then_inc(kq_loaded[j], 16)
                src = v_scr[bass.ds(g, 1), :, :].rearrange("a p (t c) -> (a p) t c", c=P)[:, :, j * HD:(j + 1) * HD]
                sp.dma_start(vh[j][:, :, :], src).then_inc(v_loaded[j], 16)

            def load_negmax(g, j):
                n, _ = transposed_unit(*head(g, j, -1))
                sp.wait_ge(mx_free, n + 1)
                sp.dma_start(qp[j][PACK:PACK + 1, :].bitcast(F32), neg_max[j][:, :]).then_inc(negmax_loaded[j], 16)

            def invert_sums(g, j):
                h = number(g, j)
                sp.wait_ge(sums_taken, h + 1)
                for b in range(QB):
                    sp.dma_start(sums_q[b * HD:(b + 1) * HD, :], sums_b[b * HD:b * HD + 1, :]) \
                        .then_inc(sums_spread, 16)
                sp.wait_ge(recip_done, h + 1)
                sp.dma_start(recip_scr.rearrange("(p c) -> p c", p=P), recip_q[:, :]).then_inc(recip_stored, 16)
                sp.wait_ge(recip_stored, 16 * (h + 1))
                for b in range(QB):
                    sp.dma_start(recip_b[b * HD:(b + 1) * HD, :],
                                 recip_scr[b * NQ:(b + 1) * NQ].partition_broadcast(HD)).then_inc(recip_loaded, 16)

            def store_ctx(g, j):
                h = number(g, j)
                sp.wait_ge(ctx_ready, h + 1)
                for b in range(QB):
                    sp.dma_start(cz_scr[bass.ds(h * HD, HD), b * NQ:(b + 1) * NQ],
                                 out_ctx[j % 2][b * HD:(b + 1) * HD, :]).then_inc(ctx_stored[j % 2], 16)

            for j in range(SLOTS):
                load(0, j)
            sp.dma_start(w_early[:, :, :], w2[0:EARLY * P, :].rearrange("(k p) n -> p k n", p=P)) \
                .then_inc(early_loaded, 16)

            def period(g, j, attends, before):
                gb, jb = head(g, j, -1)
                if before:
                    sp.wait_ge(pv_done, 16 * number(g, j))
                    if not isinstance(gb, int) or gb < LAST[0]:
                        load(gb + 1, jb)
                    invert_sums(gb, jb)
                    store_ctx(gb, jb)
                if not is_last(g, j):
                    load_negmax(*head(g, j, 1))

            scheduled(sp, period)
            store_ctx(*LAST)
            for s in range(2):
                sp.wait_ge(ctx_stored[s], 16 * QB * HEADS // 2)

        @block.gpsimd
        def _(pool):
            pool.memset(ident[:, :], 0.0).then_inc(ident_done, 1)
            pool.wait_ge(ident_done, 1)
            pool.affine_select(out=ident[:, :], in_=ident[:, :], compare_op=ALU.not_equal, fill=1.0,
                               base=0, pattern=[[-1, P]], channel_multiplier=1).then_inc(ident_done, 1)
            pool.memset(ones[:, :], 1.0).then_inc(ones_done, 1)
            for s in range(SLOTS):
                pool.wait_ge(ones_done, s + 1)
                pool.memset(kp[s][PACK:PACK + 1, :].bitcast(F32), 1.0).then_inc(ones_done, 1)

            pool.wait_ge(ones_done, SLOTS + 1)

            def period(g, j):
                h = number(g, j)
                acc = psum_p[j % 2]
                mine, by_dve, _ = tiles(g, j)
                wait(pool, sum_ready, h - 1)
                for n, t in enumerate(mine[1:]):
                    pool.wait_ge(exp_done, 64 * h + 4 * t + 4)
                    if n:
                        pool.wait_ge(pool_done, pool_count(g, j, mine[n]))
                    pool.tensor_tensor(acc[:, :], (acc if n else probs[0])[:, :], probs[t % RING][:, :], ALU.add) \
                        .then_inc(pool_done, 1)
                pool.wait_ge(added, added_count(g, j, by_dve[-1]))
                pool.wait_ge(pool_done, pool_count(g, j, mine[-1]))
                pool.tensor_tensor(acc[:, :], acc[:, :], psum_d[:, :], ALU.add).then_inc(pool_done, 1)

            for j in range(SLOTS):
                period(0, j)
            with pool.Fori(1, LAST[0]) as g:
                for j in range(SLOTS):
                    period(g, j)
            for j in range(SLOTS):
                period(LAST[0], j)

        @block.tensor
        def _(pe):
            pe.wait_ge(ident_done, 2)
            pe.wait_ge(ones_done, 1 + SLOTS)

            def scores_t(g, j, t, b):
                h = number(g, j)
                banks = QB if is_last(g, j) and t else ST_BANKS
                if t or b < ST_BANKS or not is_last(g, j):
                    wait(pe, exp_done, 64 * h + 4 * t + b - banks + 1)
                pe.matmul(ps[:, st_bank(g, j, b), :], kp[j][0:PACK + 1, t * P:(t + 1) * P],
                          qp[j][0:PACK + 1, b * NQ:(b + 1) * NQ], start=True, stop=True).then_inc(st_ready, 1)

            def scores(g, j, t, b):
                gn, jn, tn = target(g, j, t)
                n, bank = unit(g, j, t, b)
                wait(pe, mx_free, n - MAX_BANKS + 1)
                if tn == 0 and b == 0:
                    pe.wait_ge(kq_loaded[jn], 16 * 6 * (gn + 1))
                pe.matmul(ps[:, MAX_BANK + bank, :], qp[jn][0:PACK, tn * P:(tn + 1) * P],
                          kp[jn][0:PACK, b * NQ:(b + 1) * NQ], start=True, stop=True).then_inc(mx_ready, 1)

            def transpose_max(g, j):
                gn, jn = head(g, j, 1)
                n, bank = transposed_unit(g, j)
                pe.wait_ge(rowmax_ready, number(gn, jn) + 1)
                pe.wait_ge(mx_free, n - MAX_BANKS + 1)
                pe.transpose(ps[0:TT, MAX_BANK + bank, 0:P], row_max[jn % 2][:, :], ident[:, :]).then_inc(mx_ready, 1)

            def values(g, j, t):
                h = number(g, j)
                pe.wait_ge(exp_done, 64 * h + 4 * t + 4)
                if t == 0:
                    pe.wait_ge(v_loaded[j], 16 * (g + 1))
                    wait(pe, raw_done, h)
                for b in range(QB):
                    last = pe.matmul(ps[b * HD:(b + 1) * HD, PV_BANK, :], vh[j][:, t, :],
                                     probs[t % RING][:, b * NQ:(b + 1) * NQ], start=(t == 0), stop=(t == TT - 1))
                if t not in tiles(g, j)[2]:
                    last.then_inc(pv_done, 1)

            def sums(g, j, t):
                mine = tiles(g, j)[2]
                if t not in mine:
                    return
                if t == mine[0]:
                    wait(pe, sums_taken, number(g, j))
                for b in range(QB):
                    last = pe.matmul(ps[b * HD:(b + 1) * HD, SUM_BANK, :], ones[:, :],
                                     probs[t % RING][:, b * NQ:(b + 1) * NQ], start=(t == mine[0]), stop=False)
                last.then_inc(pv_done, 1)

            def pool_sums(g, j):
                h = number(g, j)
                pe.wait_ge(pool_done, POOL_OPS * h + len(tiles(g, j)[0]))
                for b in range(QB):
                    last = pe.matmul(ps[b * HD:(b + 1) * HD, SUM_BANK, :], ones[:, :],
                                     psum_p[j % 2][:, b * NQ:(b + 1) * NQ], start=False, stop=True)
                last.then_inc(sum_ready, 1)

            def period(g, j, attends, has_before):
                gb, jb = head(g, j, -1)
                if attends:
                    pe.wait_ge(negmax_loaded[j], 16 * (g + 1))
                for t in range(0 if attends else -LEAD, TT):
                    late = (gb, jb, TT - 1) if t == 0 else (g, j, t - 1)
                    has_late = has_before if t == 0 else attends
                    for half in range(2):
                        for own, b in ((False, 0), (True, 0), (False, 1), (True, 1)) if half == 0 else \
                                ((True, 2), (False, 2), (True, 3), (False, 3)):
                            if own and attends:
                                scores_t(g, j, t, b)
                            if not own and has_maxima(g, j, t):
                                scores(g, j, t, b)
                        if half == (1 if is_last(g, j) else 0) and has_late:
                            values(*late)
                        if half == 1 and has_late:
                            sums(*late)
                        if half == 1 and t == POOL_SUMS_AT and has_before:
                            pool_sums(gb, jb)
                    if t == TRANSPOSED_AT and not is_last(g, j):
                        transpose_max(g, j)

            scheduled(pe, period)
            values(*LAST, TT - 1)
            sums(*LAST, TT - 1)
            pool_sums(*LAST)

        @block.scalar
        def _(act):
            def take_raw(g, j):
                h = number(g, j)
                act.wait_ge(pv_done, 16 * (h + 1))
                wait(act, ctx_ready, h - 1)
                act.activation(raw_ctx[j % 2][:, :], ps[:, PV_BANK, :], ACT.Copy).then_inc(raw_done, 1)

            def take_sums(g, j):
                h = number(g, j)
                act.wait_ge(sum_ready, h + 1)
                wait(act, sums_spread, 16 * QB * h)
                act.activation(sums_b[:, :], ps[:, SUM_BANK, :], ACT.Copy).then_inc(sums_taken, 1)

            def period(g, j, has_before=True):
                h = number(g, j)
                for t in range(TT):
                    gr, jr = (g, j) if t >= RING else head(g, j, -1)
                    tr = (t - RING) % TT
                    if has_before or t >= RING:
                        act.wait_ge(pv_done, 16 * h + t - RING + 1)
                        if tr in tiles(gr, jr)[0]:
                            act.wait_ge(pool_done, pool_count(gr, jr, tr))
                        if tr in tiles(gr, jr)[1]:
                            act.wait_ge(added, added_count(gr, jr, tr))
                    for b in range(QB):
                        act.wait_ge(st_ready, 64 * h + 4 * t + b + 1)
                        act.activation(probs[t % RING][:, b * NQ:(b + 1) * NQ], ps[:, st_bank(g, j, b), :],
                                       ACT.Exp, scale=SCALE).then_inc(exp_done, 1)
                        if t == 0 and b == 3 and has_before:
                            take_raw(*head(g, j, -1))
                        if t == TAKE_SUMS_AT and b == 3 and has_before:
                            take_sums(*head(g, j, -1))

            for j in range(SLOTS):
                period(0, j, j > 0)
            with act.Fori(1, LAST[0]) as g:
                for j in range(SLOTS):
                    period(g, j)
            for j in range(SLOTS):
                period(LAST[0], j)
            take_raw(*LAST)

        @block.vector
        def _(dve):
            def take_max(g, j, t, b):
                gn, jn, tn = target(g, j, t)
                n, bank = unit(g, j, t, b)
                dve.wait_ge(mx_ready, n + 1)
                dve.tensor_reduce(part_max[jn % 2][:, tn, b:b + 1], ps[:, MAX_BANK + bank, :], AX_X, ALU.max) \
                    .then_inc(mx_free, 1)

            def take_transposed(g, j):
                gn, jn = head(g, j, 1)
                n, bank = transposed_unit(g, j)
                wait(dve, negmax_loaded[jn], 16 * gn)
                dve.wait_ge(mx_ready, n + 1)
                dve.tensor_scalar(neg_max[jn][:, :].bitcast(F32R), ps[0:TT, MAX_BANK + bank, 0:P], -1.0, None,
                                  ALU.mult).then_inc(mx_free, 1)

            def reciprocal(g, j):
                h = number(g, j)
                dve.wait_ge(sums_spread, 16 * QB * (h + 1))
                wait(dve, recip_stored, 16 * h)
                dve.reciprocal(recip_q[:, :], sums_q[:, :]).then_inc(recip_done, 1)

            def add_tile(g, j, n, part):
                h = number(g, j)
                c = slice(part * NQ, (part + 1) * NQ)
                a, b = tiles(g, j)[1][n:n + 2]
                dve.wait_ge(exp_done, 64 * h + 4 * b + 4)
                if n:
                    dve.wait_ge(added, DVE_OPS * h + QB * (n - 1) + part + 1)
                else:
                    wait(dve, pool_done, POOL_OPS * h)
                dve.tensor_tensor(psum_d[:, c], (psum_d if n else probs[a % RING])[:, c],
                                  probs[b % RING][:, c], ALU.add).then_inc(added, 1)

            def normalise(g, j):
                h = number(g, j)
                dve.wait_ge(raw_done, h + 1)
                if is_last(g, j):
                    dve.wait_ge(sum_ready, h + 1)
                    dve.wait_ge(ctx_ready, h)
                    dve.reciprocal(recip_b[:, :], ps[:, SUM_BANK, :]).then_inc(recip_done, 1)
                    dve.wait_ge(recip_done, h + 1)
                else:
                    dve.wait_ge(recip_loaded, 16 * QB * (h + 1))
                wait(dve, ctx_stored[j % 2], 16 * QB * (2 * g + j // 2))
                dve.tensor_tensor(out_ctx[j % 2][:, :], raw_ctx[j % 2][:, :], recip_b[:, :], ALU.mult) \
                    .then_inc(ctx_ready, 1)

            def row_maxima(g, j):
                gn, jn = head(g, j, 1)
                n, _ = unit(g, j, TRANSPOSED_AT - 1, QB - 1)
                dve.wait_ge(mx_free, n + 1)
                dve.tensor_reduce(row_max[jn % 2][:, :], part_max[jn % 2][:, :, :], AX_X, ALU.max) \
                    .then_inc(rowmax_ready, 1)

            def period(g, j, attends, has_before):
                last = is_last(g, j)
                for t in range(0 if attends else -LEAD, TT):
                    for b in range(QB):
                        if (t, b) in ADD_AT and attends and not last:
                            add_tile(g, j, *divmod(ADD_AT.index((t, b)), QB))
                        if has_maxima(g, j, t):
                            take_max(g, j, t, b)
                    if t == RECIPROCAL_AT and has_before:
                        reciprocal(*head(g, j, -1))
                    if t == NORMALISE_AT and has_before:
                        normalise(*head(g, j, -1))
                    if last and t in LAST_DVE_TILES[1:]:
                        for part in range(QB):
                            add_tile(g, j, LAST_DVE_TILES.index(t) - 1, part)
                    if t == TRANSPOSED_AT - 1 and not last:
                        row_maxima(g, j)
                    if t == TRANSPOSED_AT and not last:
                        take_transposed(g, j)

            scheduled(dve, period)
            normalise(*LAST)


def project_output(nc, x, w2, bias, cz_scr, w_early, early_loaded, out):
    with ExitStack() as ctx:
        def sb(name, shape, dt=F32):
            return ctx.enter_context(nc.sbuf_tensor(name, shape, dt))

        def sem(name):
            return ctx.enter_context(nc.semaphore(name))

        whi = sb("w2hi", [P, OUT_KT, D], F32R)
        wlo = sb("w2lo", [P, OUT_KT, D], F32R)
        w_late = sb("w2_late", [P, OUT_KT - EARLY, D])
        craw = sb("craw", [P, 2, OUT_KT, P])
        chi = sb("chi", [P, 2, OUT_KT, P], F32R)
        clo = sb("clo", [P, 2, OUT_KT, P], F32R)
        xt = sb("xt", [P, 2, D])
        ob = sb("ob", [P, D])
        res = sb("res", [P, 2, D])
        ps = ctx.enter_context(nc.psum_tensor("ps_c", [P, 8, NQ], F32))

        w_loaded = [sem(f"w2_loaded{k}") for k in range(EARLY, OUT_KT)]
        whi_done = sem("w2hi_done")
        wlo_done = sem("w2lo_done")
        c_loaded = [sem("c_loaded0"), sem("c_loaded1")]
        x_loaded = [sem("xc_loaded0"), sem("xc_loaded1")]
        ob_loaded = sem("ob_loaded")
        chi_done = sem("chi_done")
        clo_done = sem("clo_done")
        xb_done = sem("xb_done")
        mm_ready = sem("c_mm_ready")
        res_ready = sem("res_ready")
        out_stored = [sem("out_stored0"), sem("out_stored1")]

        FIRST_SPLITS = 4

        def raw_w(k):
            return w_early[:, k, :] if k < EARLY else w_late[:, k - EARLY, :]

        block = ctx.enter_context(nc.Block())

        @block.sync
        def _(sp):
            def load(i, u):
                tok = bass.ds((2 * i + u) * P, P)
                sp.dma_start(craw[:, u, :, :], cz_scr[:, tok].rearrange("(k p) t -> p k t", p=P)) \
                    .then_inc(c_loaded[u], 16)
                sp.dma_start(xt[:, u, :], x[tok, :]).then_inc(x_loaded[u], 16)

            load(0, 0)
            for k in range(EARLY, OUT_KT):
                sp.dma_start(w_late[:, k - EARLY, :], w2[k * P:(k + 1) * P, :]).then_inc(w_loaded[k - EARLY], 16)
            sp.dma_start(ob[:, :], bias.partition_broadcast(P)).then_inc(ob_loaded, 16)
            load(0, 1)
            with sp.Fori(0, TT // 2 - 1) as i:
                for u in range(2):
                    n = 2 * i + u + 1
                    sp.wait_ge(clo_done, n)
                    sp.wait_ge(res_ready, n)
                    load(i + 1, u)
                    sp.dma_start(out[bass.ds((2 * i + u) * P, P), :], res[:, u, :]).then_inc(out_stored[u], 16)
            for u in range(2):
                n = TT - 1 + u
                sp.wait_ge(res_ready, n)
                sp.dma_start(out[(n - 1) * P:n * P, :], res[:, u, :]).then_inc(out_stored[u], 16)
            for u in range(2):
                sp.wait_ge(out_stored[u], 16 * TT // 2)

        @block.gpsimd
        def _(pool):
            pool.wait_ge(ob_loaded, 16)
            with pool.Fori(0, TT // 2) as i:
                for u in range(2):
                    pool.wait_ge(x_loaded[u], 16 * (i + 1))
                    pool.tensor_tensor(xt[:, u, :], xt[:, u, :], ob[:, :], ALU.add).then_inc(xb_done, 1)

        @block.tensor
        def _(pe):
            def tile(i, u, first=False):
                pe.wait_ge(chi_done, 2 * i + u + 1)
                pe.wait_ge(clo_done, 2 * i + u + 1)
                wait(pe, res_ready, 2 * i + u - 1)
                n = 0
                for k in range(OUT_KT):
                    if first:
                        pe.wait_ge(whi_done, k + 1)
                        pe.wait_ge(wlo_done, k + 1)
                    for c, w in ((chi, whi), (chi, wlo), (clo, whi)):
                        for b in range(2):
                            last = pe.matmul(ps[:, 2 * u + b, :], c[:, u, k, :], w[:, k, b * NQ:(b + 1) * NQ],
                                             start=(n == 0), stop=(n == 3 * OUT_KT - 1))
                        n += 1
                last.then_inc(mm_ready, 1)

            tile(0, 0, True)
            tile(0, 1)
            with pe.Fori(1, TT // 2) as i:
                for u in range(2):
                    tile(i, u)

        @block.scalar
        def _(act):
            def split(i, u):
                act.wait_ge(c_loaded[u], 16 * (i + 1))
                wait(act, mm_ready, 2 * i + u - 1)
                act.activation(chi[:, u, :, :], craw[:, u, :, :], ACT.Copy).then_inc(chi_done, 1)

            def split_w(k):
                act.wait_ge(early_loaded if k < EARLY else w_loaded[k - EARLY], 16)
                act.activation(whi[:, k, :], raw_w(k), ACT.Copy).then_inc(whi_done, 1)

            for k in range(FIRST_SPLITS):
                split_w(k)
            split(0, 0)
            for k in range(FIRST_SPLITS, OUT_KT):
                split_w(k)
            split(0, 1)
            with act.Fori(1, TT // 2) as i:
                for u in range(2):
                    split(i, u)

        @block.vector
        def _(dve):
            def split(i, u):
                dve.wait_ge(chi_done, 2 * i + u + 1)
                dve.tensor_tensor(clo[:, u, :, :], craw[:, u, :, :], chi[:, u, :, :].bitcast(F32), ALU.subtract) \
                    .then_inc(clo_done, 1)

            def split_w(k):
                dve.wait_ge(whi_done, k + 1)
                dve.tensor_tensor(wlo[:, k, :], raw_w(k), whi[:, k, :].bitcast(F32), ALU.subtract) \
                    .then_inc(wlo_done, 1)

            def finish(i, u):
                dve.wait_ge(mm_ready, 2 * i + u + 1)
                dve.wait_ge(xb_done, 2 * i + u + 1)
                wait(dve, out_stored[u], 16 * i)
                dve.tensor_tensor(res[:, u, :], ps[:, 2 * u:2 * u + 2, :].rearrange("p b n -> p (b n)"),
                                  xt[:, u, :], ALU.add).then_inc(res_ready, 1)

            for k in range(FIRST_SPLITS):
                split_w(k)
            split(0, 0)
            for k in range(FIRST_SPLITS, OUT_KT):
                split_w(k)
            split(0, 1)
            for u in range(2):
                finish(0, u)
                split(1, u)
            with dve.Fori(1, TT // 2 - 1) as i:
                for u in range(2):
                    finish(i, u)
                    split(i + 1, u)
            for u in range(2):
                finish(TT // 2 - 1, u)


def build(nc, x, wcat, keys_t, w2, bias, out):
    qk_scr = nc.dram_tensor("qk_scr", [2, 2 * D, T], F32, kind="Internal").ap()
    v_scr = nc.dram_tensor("v_scr", [V_BLOCKS, P, T], F32, kind="Internal").ap()
    gate_scr = nc.dram_tensor("gate_scr", [EXPERTS, T], F32, kind="Internal").ap()
    recip_scr = nc.dram_tensor("recip_scr", [T], F32, kind="Internal").ap()
    cz_scr = nc.dram_tensor("cz_scr", [D + BOTTLENECK, T], F32, kind="Internal").ap()
    project_inputs(nc, x, wcat, keys_t, qk_scr, v_scr, gate_scr, cz_scr)
    with ExitStack() as ctx:
        w_early = ctx.enter_context(nc.sbuf_tensor("w2_early", [P, EARLY, D], F32))
        early_loaded = ctx.enter_context(nc.semaphore("early_loaded"))
        attend(nc, qk_scr, v_scr, recip_scr, cz_scr, w2, w_early, early_loaded)
        project_output(nc, x, w2, bias, cz_scr, w_early, early_loaded, out)


def kernel(**inputs):
    import numpy as np
    import concourse.bacc as bacc
    from concourse.bass_utils import run_bass_kernel_spmd

    x = np.ascontiguousarray(inputs["L0_attn_x"]).reshape(T, D)
    qkvw = np.asarray(inputs["L0_attn_attn_qkvw"])
    qkvb = np.asarray(inputs["L0_attn_attn_qkvb"])
    router = np.zeros((D, P), np.float32)
    router[:, :ROUTER] = np.asarray(inputs["L0_ffn_Wq_w"]).T
    cols = np.concatenate([router, qkvw, np.asarray(inputs["L0_ffn_A_w"]).T], axis=1)
    wcat = np.zeros((BLOCKS, P, WROW), np.float32)
    wcat[:, :, :KT * P] = cols.reshape(KT, P, BLOCKS, P).transpose(2, 1, 0, 3).reshape(BLOCKS, P, KT * P)
    wcat[1:Z0, :, KT * P] = qkvb.reshape(Z0 - 1, P)
    arrays = {
        "x": x,
        "wcat": wcat,
        "keys_t": np.ascontiguousarray(np.asarray(inputs["L0_ffn_keys"]).T),
        "w2": np.concatenate([np.asarray(inputs["L0_attn_attn_ow"]), np.asarray(inputs["L0_ffn_B_w"]).T], axis=0),
        "bias": np.ascontiguousarray(inputs["L0_attn_attn_ob"]),
    }
    nc = bacc.Bacc("TRN2", target_bir_lowering=False, num_devices=1)
    aps = [nc.dram_tensor(n, a.shape, F32, kind="ExternalInput").ap() for n, a in arrays.items()]
    out = nc.dram_tensor("out", [T, D], F32, kind="ExternalOutput").ap()
    build(nc, *aps, out)
    r = run_bass_kernel_spmd(nc, [arrays], core_ids=[0])
    return r.results[0]["out"].reshape(1, T, D)
```
